# Optimizing a Trainium2 kernel written in Bass

```python
import numpy as np
import jax
import jax.numpy as jnp

def _softmax(x, axis=-1):
    return jax.nn.softmax(x, axis=axis)

def _gelu(x):
    return jax.nn.gelu(x, approximate=True)

def _silu(x):
    return jax.nn.silu(x)

def _sigmoid(x):
    return jax.nn.sigmoid(x)

def _layernorm(x, axis=-1, eps=1e-05):
    m = jnp.mean(x, axis=axis, keepdims=True)
    v = jnp.var(x, axis=axis, keepdims=True)
    return (x - m) / jnp.sqrt(v + eps)

def _scatter_add(tgt, idx, src, axis=0):
    return tgt.at[idx].add(src)

def _segment_sum(src, seg, n):
    return jax.ops.segment_sum(src, seg, n)
kernel_name = 'mk_flamingo_gated_d4_seqx_r4_7c7bfb'

def setup_inputs(seed: int=0):
    np.random.seed(seed)
    _w = jnp.asarray

    def _rec_inputs():
        import jax
        import jax.numpy as jnp
        _rk = jax.random.key(seed)
        x = 7.22e-05 + 1 * jax.random.normal(jax.random.fold_in(_rk, 1), (4, 512, 256), jnp.float32)
        _lenS = 512 - jax.random.randint(jax.random.fold_in(_rk, 7), (4,), 0, max(1, 512 // 4) + 1, jnp.int32)
        _lenS2 = 1024 - jax.random.randint(jax.random.fold_in(_rk, 8), (4,), 0, max(1, 1024 // 4) + 1, jnp.int32)
        _ctx_1024P = jax.random.normal(jax.random.fold_in(_rk, 11), (4, 16, 256), jnp.float32)
        _ctx_1024c = jax.random.dirichlet(jax.random.fold_in(_rk, 511), 0.3 * jnp.ones((16,), jnp.float32), (4, 1024))
        _ctx_1024t = jnp.einsum('bsk,bkd->bsd', _ctx_1024c, _ctx_1024P)
        _ctx_1024t = _ctx_1024t * jax.lax.rsqrt(jnp.mean(jnp.square(_ctx_1024t)) + 1e-12) * 0.953939
        ctx_1024 = 4.13588e-05 + 0.999923 * (_ctx_1024t + 0.3 * jax.random.normal(jax.random.fold_in(_rk, 611), (4, 1024, 256), jnp.float32))
        _validS = jnp.arange(512)[None, :] < _lenS[:, None]
        _validS2 = jnp.arange(1024)[None, :] < _lenS2[:, None]
        _causal = jnp.tril(jnp.ones((512, 512), dtype=bool))
        mask_BxSxS2_bf1 = jnp.ones((4, 512, 1024), dtype=bool)
        _g = jax.random.normal(jax.random.fold_in(_rk, 9001), (2, 4), jnp.float32)
        _g = jnp.sign(_g) * jnp.maximum(jnp.abs(_g), 1.0) + (_g == 0) * 1.0
        g_xattn = _g[0]
        g_ffn = _g[1]
        return (x, ctx_1024, mask_BxSxS2_bf1, g_xattn, g_ffn)
    x, ctx_1024, mask_BxSxS2_bf1, g_xattn, g_ffn = _rec_inputs()

    def _L0_xattn_setup():
        import jax, jax.numpy as jnp
        import numpy as np
        D_MODEL = 256
        NUM_HEADS = 16
        DEPTH = D_MODEL // NUM_HEADS

        def _split_heads(x, B):
            return x.reshape(B, -1, NUM_HEADS, DEPTH).transpose(0, 2, 1, 3)
        key = jax.random.key(seed)
        ks = jax.random.split(key, 10)
        B, LQ, LK = (4, 512, 512)
        bound = float(np.sqrt(6.0 / (D_MODEL + D_MODEL)))

        def w(k):
            return jax.random.uniform(k, (D_MODEL, D_MODEL), jnp.float32, -bound, bound)
        return {'query': jax.random.normal(ks[0], (B, LQ, D_MODEL), jnp.float32), 'value': jax.random.normal(ks[1], (B, LK, D_MODEL), jnp.float32), 'wq': w(ks[2]), 'bq': jnp.zeros((D_MODEL,), jnp.float32), 'wk': w(ks[3]), 'bk': jnp.zeros((D_MODEL,), jnp.float32), 'wv': w(ks[4]), 'bv': jnp.zeros((D_MODEL,), jnp.float32), 'wo': w(ks[5]), 'bo': jnp.zeros((D_MODEL,), jnp.float32)}
    _L0_xattn_all = _L0_xattn_setup()
    _L0_xattn_in = {k: v for k, v in _L0_xattn_all.items() if k in ('wq', 'bq', 'wk', 'bk', 'wv', 'bv', 'wo', 'bo')}
    del _L0_xattn_all

    def _L0_ffn_setup():
        import jax, jax.numpy as jnp
        import numpy as np

        def _binarize(w):
            alpha = jax.lax.stop_gradient(jnp.mean(jnp.abs(w), axis=1, keepdims=True))
            bw = alpha * jnp.sign(w)
            return w + jax.lax.stop_gradient(bw - w)
        key = jax.random.key(seed)
        k1, k2, k3, k4, k5 = jax.random.split(key, 5)
        D, H = (256, 1024)
        x = jax.random.normal(k1, (64, 196, D), dtype=jnp.float32)
        w1 = jax.random.normal(k2, (H, D), dtype=jnp.float32) * 0.02
        b1 = jax.random.normal(k3, (H,), dtype=jnp.float32) * 0.02
        w2 = jax.random.normal(k4, (D, H), dtype=jnp.float32) * 0.02
        b2 = jax.random.normal(k5, (D,), dtype=jnp.float32) * 0.02
        return {'x': x, 'w1': w1, 'b1': b1, 'w2': w2, 'b2': b2}
    _L0_ffn_all = _L0_ffn_setup()
    _L0_ffn_in = {k: v for k, v in _L0_ffn_all.items() if k in ('w1', 'b1', 'w2', 'b2')}
    del _L0_ffn_all

    def _L1_xattn_setup():
        import jax, jax.numpy as jnp
        import numpy as np
        B, S1, S2 = (2, 512, 512)
        E = 256
        H = 16
        DH = E // H
        key = jax.random.key(seed)
        ks = jax.random.split(key, 12)
        s = 0.02
        return {'query': jax.random.normal(ks[0], (B, S1, E), jnp.float32), 'key': jax.random.normal(ks[1], (B, S2, E), jnp.float32), 'value': jax.random.normal(ks[2], (B, S2, E), jnp.float32), 'attention_mask': jnp.ones((B, S1, S2), dtype=bool), 'Wq': jax.random.normal(ks[3], (H, E, DH), jnp.float32) * s, 'bq': jax.random.normal(ks[4], (H, DH), jnp.float32) * s, 'Wk': jax.random.normal(ks[5], (H, E, DH), jnp.float32) * s, 'bk': jax.random.normal(ks[6], (H, DH), jnp.float32) * s, 'Wv': jax.random.normal(ks[7], (H, E, DH), jnp.float32) * s, 'bv': jax.random.normal(ks[8], (H, DH), jnp.float32) * s, 'Wo': jax.random.normal(ks[9], (H * DH, E), jnp.float32) * s, 'bo': jax.random.normal(ks[10], (E,), jnp.float32) * s}
    _L1_xattn_all = _L1_xattn_setup()
    _L1_xattn_in = {k: v for k, v in _L1_xattn_all.items() if k in ('Wq', 'bq', 'Wk', 'bk', 'Wv', 'bv', 'Wo', 'bo')}
    del _L1_xattn_all

    def _L1_ffn_setup():
        import jax, jax.numpy as jnp
        import numpy as np
        FEATURES = 256
        D_IN = 256

        def fp8_gemm_optimized(x, input_scale, kernel, kernel_scale):
            s_in = input_scale[0]
            s_k = kernel_scale[0]
            x_q = (x.astype(jnp.float32) / s_in).astype(jnp.float8_e4m3fn)
            k_q = (kernel.astype(jnp.float32) / s_k).astype(jnp.float8_e4m3fn)
            y = jnp.dot(x_q.astype(jnp.float32), k_q.astype(jnp.float32), preferred_element_type=jnp.float32)
            return y * (s_in * s_k)
        key = jax.random.key(seed)
        kx, kk, kb = jax.random.split(key, 3)
        x = jax.random.normal(kx, (4, 2048, D_IN), dtype=jnp.float32)
        limit = np.sqrt(6.0 / (D_IN + FEATURES)).astype(np.float32)
        kernel = jax.random.uniform(kk, (D_IN, FEATURES), dtype=jnp.float32, minval=-limit, maxval=limit).astype(jnp.bfloat16)
        input_scale = jnp.ones((1,), dtype=jnp.float32)
        kernel_scale = jnp.ones((1,), dtype=jnp.float32)
        bias = jnp.zeros((FEATURES,), dtype=jnp.bfloat16)
        return {'x': x, 'kernel': kernel, 'input_scale': input_scale, 'kernel_scale': kernel_scale, 'bias': bias}
    _L1_ffn_all = _L1_ffn_setup()
    _L1_ffn_in = {k: v for k, v in _L1_ffn_all.items() if k in ('kernel', 'input_scale', 'kernel_scale', 'bias')}
    del _L1_ffn_all

    def _L2_xattn_setup():
        import jax, jax.numpy as jnp
        import numpy as np
        key = jax.random.key(seed)
        k1, k2, k3, k4 = jax.random.split(key, 4)
        B, L1, L2, D = (32, 128, 128, 256)
        ix = jax.random.normal(k1, (B, L1, D), dtype=jnp.float32)
        iother = jax.random.normal(k2, (B, L2, D), dtype=jnp.float32)
        scale = 1.0 / np.sqrt(D)
        W = jax.random.uniform(k3, (D, D), dtype=jnp.float32, minval=-scale, maxval=scale)
        b = jax.random.uniform(k4, (D,), dtype=jnp.float32, minval=-scale, maxval=scale)
        return {'ix': ix, 'iother': iother, 'W': W, 'b': b}
    _L2_xattn_all = _L2_xattn_setup()
    _L2_xattn_in = {k: v for k, v in _L2_xattn_all.items() if k in ('W', 'b')}
    del _L2_xattn_all

    def _L2_ffn_setup():
        import jax, jax.numpy as jnp
        import numpy as np
        DIM = 256

        def _reference_tuple_inner(x, W_r, W_k, W_v, mu_r, mu_k):
            B, T, C = x.shape
            x_prev = jnp.concatenate([jnp.zeros((B, 1, C), x.dtype), x[:, :-1, :]], axis=1)
            xr = mu_r * x + (1.0 - mu_r) * x_prev
            xk = mu_k * x + (1.0 - mu_k) * x_prev
            r = jax.nn.sigmoid(jnp.einsum('btc,dc->btd', xr, W_r))
            k = jnp.einsum('btc,dc->btd', xk, W_k)
            k_act = jnp.square(jax.nn.relu(k))
            out = r * jnp.einsum('btc,dc->btd', k_act, W_v)
            new_state = x[:, -1, :]
            return (out, new_state)
        key = jax.random.key(seed)
        ks = jax.random.split(key, 6)
        B, T, C = (8, 512, DIM)
        x = jax.random.normal(ks[0], (B, T, C), dtype=jnp.float32)
        s = 1.0 / np.sqrt(C)
        W_r = jax.random.uniform(ks[1], (C, C), jnp.float32, -s, s)
        W_k = jax.random.uniform(ks[2], (C, C), jnp.float32, -s, s)
        W_v = jax.random.uniform(ks[3], (C, C), jnp.float32, -s, s)
        mu_r = jax.random.uniform(ks[4], (C,), jnp.float32)
        mu_k = jax.random.uniform(ks[5], (C,), jnp.float32)
        return {'x': x, 'W_r': W_r, 'W_k': W_k, 'W_v': W_v, 'mu_r': mu_r, 'mu_k': mu_k}
    _L2_ffn_all = _L2_ffn_setup()
    _L2_ffn_in = {k: v for k, v in _L2_ffn_all.items() if k in ('W_r', 'W_k', 'W_v', 'mu_r', 'mu_k')}
    del _L2_ffn_all

    def _L3_xattn_setup():
        import jax, jax.numpy as jnp
        import numpy as np
        EMBED_DIM = 256
        NUM_HEADS = 16
        HEAD_DIM = EMBED_DIM // NUM_HEADS
        B, N, M = (4, 512, 512)

        def _split_heads(x):
            b, t, _ = x.shape
            return x.reshape(b, t, NUM_HEADS, HEAD_DIM).transpose(0, 2, 1, 3)
        key = jax.random.key(seed)
        ks = jax.random.split(key, 10)
        s = 1.0 / np.sqrt(EMBED_DIM)
        return {'query_modal': jax.random.normal(ks[0], (B, N, EMBED_DIM), jnp.float32), 'key_value_modal': jax.random.normal(ks[1], (B, M, EMBED_DIM), jnp.float32), 'Wq': jax.random.normal(ks[2], (EMBED_DIM, EMBED_DIM), jnp.float32) * s, 'bq': jnp.zeros((EMBED_DIM,), jnp.float32), 'Wk': jax.random.normal(ks[3], (EMBED_DIM, EMBED_DIM), jnp.float32) * s, 'bk': jnp.zeros((EMBED_DIM,), jnp.float32), 'Wv': jax.random.normal(ks[4], (EMBED_DIM, EMBED_DIM), jnp.float32) * s, 'bv': jnp.zeros((EMBED_DIM,), jnp.float32), 'Wo': jax.random.normal(ks[5], (EMBED_DIM, EMBED_DIM), jnp.float32) * s, 'bo': jnp.zeros((EMBED_DIM,), jnp.float32)}
    _L3_xattn_all = _L3_xattn_setup()
    _L3_xattn_in = {k: v for k, v in _L3_xattn_all.items() if k in ('Wq', 'bq', 'Wk', 'bk', 'Wv', 'bv', 'Wo', 'bo')}
    del _L3_xattn_all

    def _L3_ffn_setup():
        import jax, jax.numpy as jnp
        import numpy as np
        DIM = 256
        DEPTH = 6
        HEADS = 16
        DIM_HEAD = 64
        WINDOW = 64
        INNER = HEADS * DIM_HEAD
        DIM_INNER = int(DIM * 4 * 2 / 3)
        QK_SCALE = 8.0

        def shift_tokens(t):
            a, s = jnp.split(t, 2, -1)
            s = jnp.pad(s, ((0, 0), (1, 0), (0, 0)))[:, :-1]
            return jnp.concatenate([a, s], -1)

        def l2norm(t):
            return t / jnp.maximum(jnp.linalg.norm(t, axis=-1, keepdims=True), 1e-12)

        def rotate_half(x):
            x1, x2 = jnp.split(x, 2, -1)
            return jnp.concatenate([-x2, x1], -1)

        def rotary_tables(n):
            half = jnp.arange(0, DIM_HEAD, 2, dtype=jnp.float32)
            inv_freq = 1.0 / 10000.0 ** (half / DIM_HEAD)
            t = jnp.arange(n, dtype=jnp.float32)
            freqs = t[:, None] * inv_freq[None, :]
            freqs = jnp.concatenate([freqs, freqs], -1)
            base_scale = (half + 0.4 * DIM_HEAD) / (1.4 * DIM_HEAD)
            power = (t - n // 2) / (WINDOW // 2)
            scale = base_scale[None, :] ** power[:, None]
            scale = jnp.concatenate([scale, scale], -1)
            return (freqs, scale)

        def local_attention(q, k, v):
            b, h, n, d = q.shape
            w = WINDOW
            nw = n // w
            bq = q.reshape(b, h, nw, w, d)
            bk = k.reshape(b, h, nw, w, d)
            bv = v.reshape(b, h, nw, w, d)

            def look(t):
                p = jnp.pad(t, ((0, 0), (0, 0), (1, 0), (0, 0), (0, 0)))
                return jnp.concatenate([p[:, :, :nw], p[:, :, 1:]], axis=3)
            bk2, bv2 = (look(bk), look(bv))
            seq = jnp.arange(n).reshape(nw, w)
            seq_p = jnp.pad(seq, ((1, 0), (0, 0)), constant_values=-1)
            jt = jnp.concatenate([seq_p[:nw], seq_p[1:]], axis=1)
            it = seq[:, :, None]
            jb = jt[:, None, :]
            mask = (it < jb) | (it > jb + w) | (jb == -1)
            sim = jnp.einsum('bhwie,bhwje->bhwij', bq, bk2) * QK_SCALE
            sim = jnp.where(mask, -jnp.finfo(sim.dtype).max, sim)
            attn = jax.nn.softmax(sim, -1)
            out = jnp.einsum('bhwij,bhwje->bhwie', attn, bv2)
            return out.reshape(b, h, n, d)

        def attn_layer(x, Wqkv, qs, ksc, Wo):
            b, n, _ = x.shape
            qkv = x @ Wqkv
            q, k, v = jnp.split(qkv, 3, -1)
            sh = lambda t: t.reshape(b, n, HEADS, DIM_HEAD).transpose(0, 2, 1, 3)
            q, k, v = (sh(q), sh(k), sh(v))
            q = l2norm(q) * qs
            k = l2norm(k) * ksc
            freqs, scale = rotary_tables(n)
            cos, sin = (jnp.cos(freqs), jnp.sin(freqs))
            q = q * cos * scale + rotate_half(q) * sin * scale
            inv = 1.0 / scale
            k = k * cos * inv + rotate_half(k) * sin * inv
            out = local_attention(q, k, v)
            out = out.transpose(0, 2, 1, 3).reshape(b, n, INNER)
            return out @ Wo

        def ffn_layer(x, g, bln, W1, b1, W2, b2):
            mu = x.mean(-1, keepdims=True)
            var = ((x - mu) ** 2).mean(-1, keepdims=True)
            xn = (x - mu) / jnp.sqrt(var + 1e-05) * g + bln
            hg = xn @ W1 + b1
            a, gate = jnp.split(hg, 2, -1)
            return a * jax.nn.gelu(gate, approximate=False) @ W2 + b2
        key = jax.random.key(seed)
        ks = jax.random.split(key, 8)
        B, N = (2, 512)
        init = lambda k, shape: jax.random.normal(k, shape, jnp.float32) * 0.02
        return {'x': jax.random.normal(ks[0], (B, N, DIM), jnp.float32), 'Wqkv': init(ks[1], (DEPTH, DIM, 3 * INNER)), 'q_scale': jnp.ones((DEPTH, DIM_HEAD), jnp.float32), 'k_scale': jnp.ones((DEPTH, DIM_HEAD), jnp.float32), 'Wo': init(ks[2], (DEPTH, INNER, DIM)), 'ln_g': jnp.ones((DEPTH, DIM), jnp.float32), 'ln_b': jnp.zeros((DEPTH, DIM), jnp.float32), 'W1': init(ks[3], (DEPTH, DIM, 2 * DIM_INNER)), 'b1': jnp.zeros((DEPTH, 2 * DIM_INNER), jnp.float32), 'W2': init(ks[4], (DEPTH, DIM_INNER, DIM)), 'b2': jnp.zeros((DEPTH, DIM), jnp.float32)}
    _L3_ffn_all = _L3_ffn_setup()
    _L3_ffn_in = {k: v for k, v in _L3_ffn_all.items() if k in ('Wqkv', 'q_scale', 'k_scale', 'Wo', 'ln_g', 'ln_b', 'W1', 'b1', 'W2', 'b2')}
    del _L3_ffn_all
    return {'x': x, 'ctx_1024': ctx_1024, 'mask_BxSxS2_bf1': mask_BxSxS2_bf1, 'g_xattn': g_xattn, 'g_ffn': g_ffn, 'L0_xattn_wq': _L0_xattn_in['wq'], 'L0_xattn_bq': _L0_xattn_in['bq'], 'L0_xattn_wk': _L0_xattn_in['wk'], 'L0_xattn_bk': _L0_xattn_in['bk'], 'L0_xattn_wv': _L0_xattn_in['wv'], 'L0_xattn_bv': _L0_xattn_in['bv'], 'L0_xattn_wo': _L0_xattn_in['wo'], 'L0_xattn_bo': _L0_xattn_in['bo'], 'L0_ffn_w1': _L0_ffn_in['w1'], 'L0_ffn_b1': _L0_ffn_in['b1'], 'L0_ffn_w2': _L0_ffn_in['w2'], 'L0_ffn_b2': _L0_ffn_in['b2'], 'L1_xattn_Wq': _L1_xattn_in['Wq'], 'L1_xattn_bq': _L1_xattn_in['bq'], 'L1_xattn_Wk': _L1_xattn_in['Wk'], 'L1_xattn_bk': _L1_xattn_in['bk'], 'L1_xattn_Wv': _L1_xattn_in['Wv'], 'L1_xattn_bv': _L1_xattn_in['bv'], 'L1_xattn_Wo': _L1_xattn_in['Wo'], 'L1_xattn_bo': _L1_xattn_in['bo'], 'L1_ffn_kernel': _L1_ffn_in['kernel'], 'L1_ffn_input_scale': _L1_ffn_in['input_scale'], 'L1_ffn_kernel_scale': _L1_ffn_in['kernel_scale'], 'L1_ffn_bias': _L1_ffn_in['bias'], 'L2_xattn_W': _L2_xattn_in['W'], 'L2_xattn_b': _L2_xattn_in['b'], 'L2_ffn_W_r': _L2_ffn_in['W_r'], 'L2_ffn_W_k': _L2_ffn_in['W_k'], 'L2_ffn_W_v': _L2_ffn_in['W_v'], 'L2_ffn_mu_r': _L2_ffn_in['mu_r'], 'L2_ffn_mu_k': _L2_ffn_in['mu_k'], 'L3_xattn_Wq': _L3_xattn_in['Wq'], 'L3_xattn_bq': _L3_xattn_in['bq'], 'L3_xattn_Wk': _L3_xattn_in['Wk'], 'L3_xattn_bk': _L3_xattn_in['bk'], 'L3_xattn_Wv': _L3_xattn_in['Wv'], 'L3_xattn_bv': _L3_xattn_in['bv'], 'L3_xattn_Wo': _L3_xattn_in['Wo'], 'L3_xattn_bo': _L3_xattn_in['bo'], 'L3_ffn_Wqkv': _L3_ffn_in['Wqkv'], 'L3_ffn_q_scale': _L3_ffn_in['q_scale'], 'L3_ffn_k_scale': _L3_ffn_in['k_scale'], 'L3_ffn_Wo': _L3_ffn_in['Wo'], 'L3_ffn_ln_g': _L3_ffn_in['ln_g'], 'L3_ffn_ln_b': _L3_ffn_in['ln_b'], 'L3_ffn_W1': _L3_ffn_in['W1'], 'L3_ffn_b1': _L3_ffn_in['b1'], 'L3_ffn_W2': _L3_ffn_in['W2'], 'L3_ffn_b2': _L3_ffn_in['b2']}

def reference(x, ctx_1024, mask_BxSxS2_bf1, g_xattn, g_ffn, L0_xattn_wq, L0_xattn_bq, L0_xattn_wk, L0_xattn_bk, L0_xattn_wv, L0_xattn_bv, L0_xattn_wo, L0_xattn_bo, L0_ffn_w1, L0_ffn_b1, L0_ffn_w2, L0_ffn_b2, L1_xattn_Wq, L1_xattn_bq, L1_xattn_Wk, L1_xattn_bk, L1_xattn_Wv, L1_xattn_bv, L1_xattn_Wo, L1_xattn_bo, L1_ffn_kernel, L1_ffn_input_scale, L1_ffn_kernel_scale, L1_ffn_bias, L2_xattn_W, L2_xattn_b, L2_ffn_W_r, L2_ffn_W_k, L2_ffn_W_v, L2_ffn_mu_r, L2_ffn_mu_k, L3_xattn_Wq, L3_xattn_bq, L3_xattn_Wk, L3_xattn_bk, L3_xattn_Wv, L3_xattn_bv, L3_xattn_Wo, L3_xattn_bo, L3_ffn_Wqkv, L3_ffn_q_scale, L3_ffn_k_scale, L3_ffn_Wo, L3_ffn_ln_g, L3_ffn_ln_b, L3_ffn_W1, L3_ffn_b1, L3_ffn_W2, L3_ffn_b2):
    import jax
    import jax.numpy as jnp

    def _L0_xattn_ref(query, value, wq, bq, wk, bk, wv, bv, wo, bo):
        import jax, jax.numpy as jnp
        import numpy as np
        D_MODEL = 256
        NUM_HEADS = 16
        DEPTH = D_MODEL // NUM_HEADS

        def _split_heads(x, B):
            return x.reshape(B, -1, NUM_HEADS, DEPTH).transpose(0, 2, 1, 3)
        B = query.shape[0]
        q = _split_heads(query @ wq.T + bq, B)
        k = _split_heads(value @ wk.T + bk, B)
        v = _split_heads(value @ wv.T + bv, B)
        scale = jnp.sqrt(jnp.asarray(DEPTH, dtype=q.dtype))
        scores = jnp.einsum('bhqd,bhkd->bhqk', q, k) / scale
        attn = jax.nn.softmax(scores, axis=-1)
        ctx = jnp.einsum('bhqk,bhkd->bhqd', attn, v)
        ctx = ctx.transpose(0, 2, 1, 3).reshape(B, -1, D_MODEL)
        return ctx @ wo.T + bo

    def _L0_ffn_ref(x, w1, b1, w2, b2):
        import jax, jax.numpy as jnp
        import numpy as np

        def _binarize(w):
            alpha = jax.lax.stop_gradient(jnp.mean(jnp.abs(w), axis=1, keepdims=True))
            bw = alpha * jnp.sign(w)
            return w + jax.lax.stop_gradient(bw - w)
        bw1 = _binarize(w1)
        h = jnp.einsum('bsd,hd->bsh', x, bw1) + b1
        h = jax.nn.gelu(h, approximate=False)
        bw2 = _binarize(w2)
        out = jnp.einsum('bsh,dh->bsd', h, bw2) + b2
        return out

    def _L1_xattn_ref(query, key, value, attention_mask, Wq, bq, Wk, bk, Wv, bv, Wo, bo):
        import jax, jax.numpy as jnp
        import numpy as np
        B, S1, S2 = (2, 512, 512)
        E = 256
        H = 16
        DH = E // H
        q = jnp.einsum('bse,hed->bhsd', query, Wq) + bq[None, :, None, :]
        k = jnp.einsum('bte,hed->bhtd', key, Wk) + bk[None, :, None, :]
        v = jnp.einsum('bte,hed->bhtd', value, Wv) + bv[None, :, None, :]
        scale = 1.0 / jnp.sqrt(jnp.asarray(DH, q.dtype))
        scores = jnp.einsum('bhsd,bhtd->bhst', q, k) * scale
        scores = jnp.where(attention_mask[:, None, :, :], scores, -jnp.inf)
        weights = jax.nn.softmax(scores, axis=-1)
        attn = jnp.einsum('bhst,bhtd->bhsd', weights, v)
        concat = attn.transpose(0, 2, 1, 3).reshape(query.shape[0], query.shape[1], H * DH)
        return concat @ Wo + bo

    def _L1_ffn_ref(x, kernel, input_scale, kernel_scale, bias):
        import jax, jax.numpy as jnp
        import numpy as np
        FEATURES = 256
        D_IN = 256

        def fp8_gemm_optimized(x, input_scale, kernel, kernel_scale):
            s_in = input_scale[0]
            s_k = kernel_scale[0]
            x_q = (x.astype(jnp.float32) / s_in).astype(jnp.float8_e4m3fn)
            k_q = (kernel.astype(jnp.float32) / s_k).astype(jnp.float8_e4m3fn)
            y = jnp.dot(x_q.astype(jnp.float32), k_q.astype(jnp.float32), preferred_element_type=jnp.float32)
            return y * (s_in * s_k)
        dtype = jnp.bfloat16
        x = x.astype(dtype)
        orig_shape = x.shape
        x2 = x.reshape(-1, x.shape[-1])
        y = fp8_gemm_optimized(x2, input_scale, kernel, kernel_scale)
        y = y.astype(dtype) + bias
        return y.reshape(orig_shape[:-1] + (FEATURES,))

    def _L2_xattn_ref(ix, iother, W, b):
        import jax, jax.numpy as jnp
        import numpy as np
        ex = jnp.einsum('bld,ed->ble', ix, W) + b
        eother = jnp.einsum('bld,ed->ble', iother, W) + b
        scores = jnp.einsum('bld,bmd->blm', ex, eother)
        attn = jax.nn.softmax(scores, axis=-1)
        aligned = jnp.einsum('blm,bmd->bld', attn, iother)
        return aligned

    def _L2_ffn_ref(x, W_r, W_k, W_v, mu_r, mu_k):
        import jax, jax.numpy as jnp
        import numpy as np
        DIM = 256

        def _reference_tuple_inner(x, W_r, W_k, W_v, mu_r, mu_k):
            B, T, C = x.shape
            x_prev = jnp.concatenate([jnp.zeros((B, 1, C), x.dtype), x[:, :-1, :]], axis=1)
            xr = mu_r * x + (1.0 - mu_r) * x_prev
            xk = mu_k * x + (1.0 - mu_k) * x_prev
            r = jax.nn.sigmoid(jnp.einsum('btc,dc->btd', xr, W_r))
            k = jnp.einsum('btc,dc->btd', xk, W_k)
            k_act = jnp.square(jax.nn.relu(k))
            out = r * jnp.einsum('btc,dc->btd', k_act, W_v)
            new_state = x[:, -1, :]
            return (out, new_state)
        return _reference_tuple_inner(x, W_r, W_k, W_v, mu_r, mu_k)[0]

    def _L3_xattn_ref(query_modal, key_value_modal, Wq, bq, Wk, bk, Wv, bv, Wo, bo):
        import jax, jax.numpy as jnp
        import numpy as np
        EMBED_DIM = 256
        NUM_HEADS = 16
        HEAD_DIM = EMBED_DIM // NUM_HEADS
        B, N, M = (4, 512, 512)

        def _split_heads(x):
            b, t, _ = x.shape
            return x.reshape(b, t, NUM_HEADS, HEAD_DIM).transpose(0, 2, 1, 3)
        q = _split_heads(query_modal @ Wq.T + bq)
        k = _split_heads(key_value_modal @ Wk.T + bk)
        v = _split_heads(key_value_modal @ Wv.T + bv)
        scale = HEAD_DIM ** (-0.5)
        scores = jnp.einsum('bhnd,bhmd->bhnm', q, k) * scale
        attn = jax.nn.softmax(scores, axis=-1)
        x = jnp.einsum('bhnm,bhmd->bhnd', attn, v)
        x = x.transpose(0, 2, 1, 3).reshape(query_modal.shape)
        return x @ Wo.T + bo

    def _L3_ffn_ref(x, Wqkv, q_scale, k_scale, Wo, ln_g, ln_b, W1, b1, W2, b2):
        import jax, jax.numpy as jnp
        import numpy as np
        DIM = 256
        DEPTH = 6
        HEADS = 16
        DIM_HEAD = 64
        WINDOW = 64
        INNER = HEADS * DIM_HEAD
        DIM_INNER = int(DIM * 4 * 2 / 3)
        QK_SCALE = 8.0

        def shift_tokens(t):
            a, s = jnp.split(t, 2, -1)
            s = jnp.pad(s, ((0, 0), (1, 0), (0, 0)))[:, :-1]
            return jnp.concatenate([a, s], -1)

        def l2norm(t):
            return t / jnp.maximum(jnp.linalg.norm(t, axis=-1, keepdims=True), 1e-12)

        def rotate_half(x):
            x1, x2 = jnp.split(x, 2, -1)
            return jnp.concatenate([-x2, x1], -1)

        def rotary_tables(n):
            half = jnp.arange(0, DIM_HEAD, 2, dtype=jnp.float32)
            inv_freq = 1.0 / 10000.0 ** (half / DIM_HEAD)
            t = jnp.arange(n, dtype=jnp.float32)
            freqs = t[:, None] * inv_freq[None, :]
            freqs = jnp.concatenate([freqs, freqs], -1)
            base_scale = (half + 0.4 * DIM_HEAD) / (1.4 * DIM_HEAD)
            power = (t - n // 2) / (WINDOW // 2)
            scale = base_scale[None, :] ** power[:, None]
            scale = jnp.concatenate([scale, scale], -1)
            return (freqs, scale)

        def local_attention(q, k, v):
            b, h, n, d = q.shape
            w = WINDOW
            nw = n // w
            bq = q.reshape(b, h, nw, w, d)
            bk = k.reshape(b, h, nw, w, d)
            bv = v.reshape(b, h, nw, w, d)

            def look(t):
                p = jnp.pad(t, ((0, 0), (0, 0), (1, 0), (0, 0), (0, 0)))
                return jnp.concatenate([p[:, :, :nw], p[:, :, 1:]], axis=3)
            bk2, bv2 = (look(bk), look(bv))
            seq = jnp.arange(n).reshape(nw, w)
            seq_p = jnp.pad(seq, ((1, 0), (0, 0)), constant_values=-1)
            jt = jnp.concatenate([seq_p[:nw], seq_p[1:]], axis=1)
            it = seq[:, :, None]
            jb = jt[:, None, :]
            mask = (it < jb) | (it > jb + w) | (jb == -1)
            sim = jnp.einsum('bhwie,bhwje->bhwij', bq, bk2) * QK_SCALE
            sim = jnp.where(mask, -jnp.finfo(sim.dtype).max, sim)
            attn = jax.nn.softmax(sim, -1)
            out = jnp.einsum('bhwij,bhwje->bhwie', attn, bv2)
            return out.reshape(b, h, n, d)

        def attn_layer(x, Wqkv, qs, ksc, Wo):
            b, n, _ = x.shape
            qkv = x @ Wqkv
            q, k, v = jnp.split(qkv, 3, -1)
            sh = lambda t: t.reshape(b, n, HEADS, DIM_HEAD).transpose(0, 2, 1, 3)
            q, k, v = (sh(q), sh(k), sh(v))
            q = l2norm(q) * qs
            k = l2norm(k) * ksc
            freqs, scale = rotary_tables(n)
            cos, sin = (jnp.cos(freqs), jnp.sin(freqs))
            q = q * cos * scale + rotate_half(q) * sin * scale
            inv = 1.0 / scale
            k = k * cos * inv + rotate_half(k) * sin * inv
            out = local_attention(q, k, v)
            out = out.transpose(0, 2, 1, 3).reshape(b, n, INNER)
            return out @ Wo

        def ffn_layer(x, g, bln, W1, b1, W2, b2):
            mu = x.mean(-1, keepdims=True)
            var = ((x - mu) ** 2).mean(-1, keepdims=True)
            xn = (x - mu) / jnp.sqrt(var + 1e-05) * g + bln
            hg = xn @ W1 + b1
            a, gate = jnp.split(hg, 2, -1)
            return a * jax.nn.gelu(gate, approximate=False) @ W2 + b2
        for i in range(DEPTH):
            x = attn_layer(shift_tokens(x), Wqkv[i], q_scale[i], k_scale[i], Wo[i]) + x
            x = ffn_layer(shift_tokens(x), ln_g[i], ln_b[i], W1[i], b1[i], W2[i], b2[i]) + x
        return x
    x = x + jnp.tanh(g_xattn[0]) * _L0_xattn_ref(_layernorm(x, axis=-1), ctx_1024, L0_xattn_wq, L0_xattn_bq, L0_xattn_wk, L0_xattn_bk, L0_xattn_wv, L0_xattn_bv, L0_xattn_wo, L0_xattn_bo)
    x = x + jnp.tanh(g_ffn[0]) * _L0_ffn_ref(_layernorm(x, axis=-1), L0_ffn_w1, L0_ffn_b1, L0_ffn_w2, L0_ffn_b2)
    x = x + jnp.tanh(g_xattn[1]) * _L1_xattn_ref(_layernorm(x, axis=-1), ctx_1024, ctx_1024, mask_BxSxS2_bf1, L1_xattn_Wq, L1_xattn_bq, L1_xattn_Wk, L1_xattn_bk, L1_xattn_Wv, L1_xattn_bv, L1_xattn_Wo, L1_xattn_bo)
    x = x + jnp.tanh(g_ffn[1]) * _L1_ffn_ref(_layernorm(x, axis=-1), L1_ffn_kernel, L1_ffn_input_scale, L1_ffn_kernel_scale, L1_ffn_bias)
    x = x + jnp.tanh(g_xattn[2]) * _L2_xattn_ref(_layernorm(x, axis=-1), ctx_1024, L2_xattn_W, L2_xattn_b)
    x = x + jnp.tanh(g_ffn[2]) * _L2_ffn_ref(_layernorm(x, axis=-1), L2_ffn_W_r, L2_ffn_W_k, L2_ffn_W_v, L2_ffn_mu_r, L2_ffn_mu_k)
    x = x + jnp.tanh(g_xattn[3]) * _L3_xattn_ref(_layernorm(x, axis=-1), ctx_1024, L3_xattn_Wq, L3_xattn_bq, L3_xattn_Wk, L3_xattn_bk, L3_xattn_Wv, L3_xattn_bv, L3_xattn_Wo, L3_xattn_bo)
    x = x + jnp.tanh(g_ffn[3]) * _L3_ffn_ref(_layernorm(x, axis=-1), L3_ffn_Wqkv, L3_ffn_q_scale, L3_ffn_k_scale, L3_ffn_Wo, L3_ffn_ln_g, L3_ffn_ln_b, L3_ffn_W1, L3_ffn_b1, L3_ffn_W2, L3_ffn_b2)
    return x

_drawn_inputs = setup_inputs


def setup_inputs(seed=0):
    import zlib

    import numpy as np

    out = dict(_drawn_inputs(seed))
    spreads = {'L0_xattn_bq': (0.0, 0.1),
     'L0_xattn_bk': (0.0, 0.8),
     'L0_xattn_bv': (0.0, 0.1),
     'L0_xattn_bo': (0.0, 0.1),
     'L1_ffn_bias': (0.0, 0.1),
     'L3_xattn_bq': (0.0, 0.735),
     'L3_xattn_bk': (0.0, 0.8),
     'L3_xattn_bv': (0.0, 0.1),
     'L3_xattn_bo': (0.0, 0.1),
     'L3_ffn_q_scale': (1.0, 0.6),
     'L3_ffn_k_scale': (1.0, 0.6),
     'L3_ffn_ln_g': (1.0, 0.6),
     'L3_ffn_ln_b': (0.0, 0.8),
     'L3_ffn_b1': (0.0, 0.661),
     'L3_ffn_b2': (0.0, 0.1)}
    factors = {'L0_ffn_b1': 5.01,
     'L1_xattn_Wq': 7.097,
     'L1_xattn_bq': 8.0,
     'L1_xattn_Wk': 7.418,
     'L1_xattn_bk': 8.0,
     'L1_xattn_bv': 4.198,
     'L2_ffn_W_r': 5.94,
     'L2_ffn_mu_r': 8.0,
     'L2_ffn_mu_k': 2.773}
    for name, (base, spread) in spreads.items():
        noise = np.random.default_rng([zlib.crc32(name.encode()), seed]).standard_normal(out[name].shape)
        drawn = base * np.exp(spread * noise) if base else spread * noise
        out[name] = jnp.asarray(drawn.astype(out[name].dtype))
    for name, factor in factors.items():
        out[name] = (out[name] * factor).astype(out[name].dtype)
    return out
```

```python
from contextlib import ExitStack

import numpy as np

import concourse.bass as bass
from concourse import mybir

ALU = mybir.AluOpType
ACT = mybir.ActivationFunctionType
AX = mybir.AxisListType
F32 = mybir.dt.float32
F32R = mybir.dt.float32r
BF16 = mybir.dt.bfloat16
FP8 = mybir.dt.float8e4
U8 = mybir.dt.uint8

P = 128
B, S, S2, D = 4, 512, 1024, 256
C = D // P
H = 16
HD = D // H
QT = S // P
KT = S2 // P
G4 = H // 4
FF0 = 1024 // P
PAD = 8
ROW = PAD + S
EPS = 1e-5
MASKED = -1e30
PAIRS = [(0, 0), (0, 1), (0, 2), (1, 0), (1, 1), (2, 0)]
STACK = len(PAIRS) * HD
DEPTH, LHD, WIN = 6, 64, 64
INNER = H * LHD
HID = int(D * 4 * 2 / 3)
HT = -(-HID // P)

VECS = {}
_n = 0
for _name, _w in (
    [("L0_bq", 2), ("L0_bk", 2), ("L0_bo", 2), ("L0_b1", FF0), ("L0_b2", 2),
     ("L1_bq", 2), ("L1_bk", 2), ("L1_bo", 2), ("L2_b", 2), ("mu_r", 2), ("mu_k", 2),
     ("L3_bq", 2), ("L3_bk", 2), ("L3_bo", 2), ("g_x", 4), ("g_f", 4), ("s_in", 1), ("s_k", 1)]
    + [(f"{n}{i}", w) for i in range(DEPTH)
       for n, w in (("ln_g", 2), ("ln_b", 2), ("b1a", HT), ("b1g", HT), ("b2", 2))]
):
    VECS[_name] = _n
    _n += _w
N_VECS = _n


def bc(ap, axis, n):
    dims = [list(d) for d in ap.ap]
    return bass.AP(ap.tensor, ap.offset, dims[:axis] + [[0, n]] + dims[axis:])


class Queue:

    def __init__(self, eng, sem):
        self.eng, self.sem, self.n, self.seen = eng, sem, 0, {}

    def wait(self, *marks):
        for m in marks:
            if isinstance(m, list):
                self.wait(*m)
            elif m is not None:
                sem, value = m
                if self.seen.get(id(sem), 0) < value:
                    self.eng.wait_ge(sem, value)
                    self.seen[id(sem)] = value

    def done(self, ins):
        self.n += 1
        ins.then_inc(self.sem, 1)
        return (self.sem, self.n)


class Slot:

    def __init__(self, ap, sem=None):
        self.ap, self.free, self.sem, self.n = ap, [], sem, 0

    def dma(self, ins):
        self.n += 16
        ins.then_inc(self.sem, 16)
        return (self.sem, self.n)


class Ring:

    def __init__(self, slots):
        self.slots = list(slots)
        self.low = len(self.slots)

    def take(self):
        return self.slots.pop(0)

    def give(self, slot, *marks):
        slot.free = list(marks)
        self.slots.append(slot)


class Banks:

    def __init__(self, ps):
        self.ps, self.order, self.free = ps, list(range(8)), [[] for _ in range(8)]

    def left(self, n):
        if n == 1:
            return len(self.order) > 0
        return any(b % 2 == 0 and b + 1 in self.order for b in self.order)

    def take(self, n=1):
        if n == 2:
            pairs = [b for b in range(0, 8, 2) if b in self.order and b + 1 in self.order]
            b = min(pairs, key=lambda b: max(self.order.index(b), self.order.index(b + 1)))
        else:
            single = [b for b in self.order if b ^ 1 not in self.order]
            b = (single or self.order)[0]
        for x in range(b, b + n):
            self.order.remove(x)
        s = Slot(self.ps[:, b, :] if n == 1 else self.ps[:, b:b + 2, :])
        s.bank, s.width = b, n
        s.free = [m for x in range(b, b + n) for m in self.free[x]]
        return s

    def give(self, slot, *marks):
        for x in range(slot.bank, slot.bank + slot.width):
            self.free[x] = list(marks)
            self.order.append(x)


def need(*wanted):
    while True:
        ok = True
        for w in wanted:
            if isinstance(w[0], Banks):
                banks, ones, pairs = w
                whole = sum(b in banks.order and b + 1 in banks.order for b in range(0, 8, 2))
                lone = len(banks.order) - 2 * whole
                ok &= whole >= pairs and lone + 2 * (whole - pairs) >= ones
            else:
                ok &= len(w[0].slots) >= w[1]
        if ok:
            return
        yield


def run_jobs(jobs, window):
    jobs = list(jobs)
    live = []
    stuck = 0
    while jobs or live:
        while jobs and len(live) < window:
            live.append(jobs.pop(0))
        for j in list(live):
            before = Progress.count
            try:
                next(j)
            except StopIteration:
                live.remove(j)
                Progress.count += 1
            stuck = 0 if Progress.count != before else stuck + 1
            if stuck > 50:
                raise RuntimeError("no job can go on: too few buffers")


class Progress:
    count = 0


def build(nc, a, out, stages=99, depths=DEPTH):
    ctx = ExitStack()
    with ctx:
        def sem(name):
            return ctx.enter_context(nc.semaphore(name))

        def sb(name, shape, dt=F32, where=ctx):
            return where.enter_context(nc.sbuf_tensor(name, shape, dt))

        PE = Queue(nc.tensor, sem("pe_done"))
        V = Queue(nc.vector, sem("vector_done"))
        A = Queue(nc.scalar, sem("scalar_done"))
        G = Queue(nc.gpsimd, sem("gpsimd_done"))
        SP = Queue(nc.sync, sem("sync_done"))

        def count(q, ins):
            Progress.count += 1
            return q.done(ins)

        def v_(ins): return count(V, ins)
        def a_(ins): return count(A, ins)
        def g_(ins): return count(G, ins)
        def pe_(ins): return count(PE, ins)

        tensor, vector, scalar, gpsimd, sync = nc.tensor, nc.vector, nc.scalar, nc.gpsimd, nc.sync
        psum_all = ctx.enter_context(nc.psum_tensor("psum", [P, 8, 512], F32))
        banks = Banks(psum_all)

        X = sb("x_resid", [P, C, B, ROW])
        vecs = sb("vecs", [P, N_VECS])
        gates = sb("gates", [P, 8])
        ones_mean = sb("ones_mean", [P, P])
        ident = sb("ident", [P, P])
        ident_b = sb("ident_b", [P, P], BF16)
        eps_col = sb("eps_col", [P, 2])
        small = sb("small", [P, 64])

        s_vec, s_x = sem("vecs_loaded"), sem("x_loaded")
        sync.dma_start(vecs[:, :], a["vecs"]).then_inc(s_vec, 16)
        sync.dma_start(ident[:, :], a["ident"]).then_inc(s_vec, 16)
        for c in range(C):
            sync.dma_start(X[:, c, :, PAD:ROW], a["xT"][c * P:(c + 1) * P, :, :]).then_inc(s_x, 16)
        vec_in, x_in = (s_vec, 32), (s_x, 16 * C)
        t_pad = v_(vector.memset(X[:, :, :, 0:PAD], 0.0))
        t_ones = v_(vector.memset(ones_mean[:, :], 1.0 / D))
        v_(vector.memset(eps_col[:, 0:1], EPS))
        t_const = v_(vector.memset(eps_col[:, 1:2], float(10 * np.log(2.0))))
        V.wait(vec_in)
        t_idb = v_(vector.tensor_copy(ident_b[:, :], ident[:, :]))
        A.wait(vec_in)
        t_gate = a_(scalar.activation(gates[:, 0:8], vecs[:, VECS["g_x"]:VECS["g_x"] + 8], ACT.Tanh))
        x_ready = [[x_in, t_pad] for _ in range(B)]

        def vec(name, i=0):
            return vecs[:, VECS[name] + i:VECS[name] + i + 1]

        V.wait(t_gate)
        small_at = {}

        def derived(name, width, fn):
            at = sum(w for _, w in small_at.values())
            small_at[name] = (at, width)
            return v_(fn(small[:, at:at + width]))

        def sm(name, i=0):
            at = small_at[name][0] + i
            return small[:, at:at + 1]

        V.wait(vec_in)
        v2 = lambda name, w=2: vecs[:, VECS[name]:VECS[name] + w]
        for L, gi in (("L0", 0), ("L1", 1), ("L3", 3)):
            derived(L + "_bq4", 2, lambda o, L=L: vector.tensor_scalar(o, v2(L + "_bq"), 0.25, None, ALU.mult))
            derived(L + "_gbo", 2, lambda o, L=L, gi=gi: vector.tensor_scalar(
                o, v2(L + "_bo"), gates[:, gi:gi + 1], None, ALU.mult))
        derived("L0_gb2", 2, lambda o: vector.tensor_scalar(o, v2("L0_b2"), gates[:, 4:5], None, ALU.mult))
        derived("om_r", 2, lambda o: vector.tensor_scalar(o, v2("mu_r"), -1.0, 1.0, ALU.mult, ALU.add))
        derived("om_k", 2, lambda o: vector.tensor_scalar(o, v2("mu_k"), -1.0, 1.0, ALU.mult, ALU.add))
        derived("inv_in", 1, lambda o: vector.reciprocal(o, vec("s_in")))
        derived("inv_k", 1, lambda o: vector.reciprocal(o, vec("s_k")))
        t_small = derived("s_both", 1, lambda o: vector.tensor_tensor(o, vec("s_in"), vec("s_k"), ALU.mult))
        for q in (V, A):
            q.wait(t_small, t_idb, t_const)
        PE.wait(t_ones, t_idb)

        x_kept = nc.dram_tensor("x_kept", [D, B, S], F32).ap()
        kept = [None] * B

        def tokens(b, c, shift=0):
            return X[:, c, b, PAD - shift:ROW - shift]

        def rsqrt_newton(out, var_plus, y, t):
            m = v_(var_plus(t, y))
            V.wait(m)
            m = v_(vector.tensor_tensor(t, t, y, ALU.mult))
            V.wait(m)
            m = v_(vector.tensor_scalar(t, t, -0.5, 1.5, ALU.mult, ALU.add))
            V.wait(m)
            return v_(vector.tensor_tensor(out, y, t, ALU.mult))

        def centred_rstd(b, shift, xc, work):
            yield from need((banks, 1, 0))
            mean = banks.take()
            PE.wait(x_ready[b], mean.free)
            for c in range(C):
                ins = tensor.matmul(mean.ap, ones_mean[:, :], tokens(b, c, shift * c), start=c == 0, stop=c == C - 1)
            t_mean = pe_(ins)
            yield
            V.wait(t_mean, xc.free, x_ready[b])
            for c in range(C):
                t_xc = v_(vector.tensor_tensor(xc.ap[:, c, PAD:ROW], tokens(b, c, shift * c), mean.ap, ALU.subtract))
            banks.give(mean, t_xc)
            yield from need((banks, 1, 0), (work, 2))
            sq0, sq1 = work.take(), work.take()
            A.wait(t_xc, sq0.free, sq1.free)
            for c, s in enumerate((sq0, sq1)):
                t_sq = a_(scalar.activation(s.ap, xc.ap[:, c, PAD:ROW], ACT.Square))
            var = banks.take()
            PE.wait(t_sq, var.free)
            for c, s in enumerate((sq0, sq1)):
                ins = tensor.matmul(var.ap, ones_mean[:, :], s.ap, start=c == 0, stop=c == C - 1)
            t_var = pe_(ins)
            yield
            y, t = sq0, sq1
            A.wait(t_var)
            t_y = a_(scalar.activation(y.ap, var.ap, ACT.Ln, bias=eps_col[:, 0:1]))
            A.wait(t_y)
            t_y = a_(scalar.activation(y.ap, y.ap, ACT.Exp, scale=-0.5))
            V.wait(t_y, t_var)
            t_rs = rsqrt_newton(y.ap, lambda o, i: vector.scalar_tensor_tensor(
                out=o, in0=var.ap, scalar=EPS, in1=i, op0=ALU.add, op1=ALU.mult), y.ap, t.ap)
            banks.give(var, t_rs)
            work.give(t, t_rs)
            return y, t_rs

        def layer_norm(b, xn, work):
            rstd, t_rs = yield from centred_rstd(b, 0, xn, work)
            V.wait(t_rs)
            for c in range(C):
                t = v_(vector.tensor_tensor(xn.ap[:, c, PAD:ROW], xn.ap[:, c, PAD:ROW], rstd.ap, ALU.mult))
            work.give(rstd, t)
            return t

        def first_part(p1):
            def psb(name, shape, dt=F32):
                return sb(name, shape, dt, p1)

            w_att = Slot(psb("w_att", [P, 10 * D])[:, :], sem("w_att_in"))
            w_ff = Slot(psb("w_ff", [P, 2 * FF0 * D])[:, :], sem("w_ff_in"))
            w_ffb = psb("w_ffb", [P, C, D], BF16)
            bias_b = psb("bias_b", [P, C], BF16)
            bv = psb("bv", [P, 3, D])
            ctxs = Ring(Slot(psb(f"ctx{i}", [P, C, S2])[:, :, :], sem(f"ctx_in{i}")) for i in range(1))
            norms = Ring(Slot(psb(f"xn{i}", [P, C, ROW])[:, :, :]) for i in range(3))
            works = Ring(Slot(psb(f"work{i}", [P, S])[:, :]) for i in range(6))
            parts = Ring(Slot(psb(f"parts{i}", [P, 3, S], BF16)[:, :, :], sem(f"parts_out{i}")) for i in range(3))
            stacks = Ring(Slot(psb(f"stack{i}", [P, 3 * S2])[:, :], sem(f"stack_in{i}")) for i in range(3))
            values = Ring([Slot(psb("values", [P, KT, H, 32])[:, :, :, :])])
            probs = Ring(Slot(psb(f"probs{i}", [P, 2, S])[:, :, :]) for i in range(6))
            outs = Ring(Slot(psb(f"attn{i}", [P, G4, S])[:, :, :]) for i in range(2))
            maxes = Ring(Slot(psb(f"max{i}", [P, 48])[:, :], sem(f"max_out{i}")) for i in range(4))
            shifts = Ring(Slot(psb(f"shift{i}", [16, 2, P], BF16)[:, :, :], sem(f"shift_out{i}")) for i in range(4))
            masks = Slot(psb("mask_bias", [P, QT * S2 + KT * S], BF16)[:, :])
            mask_u8 = Ring(Slot(psb(f"mask_u8{i}", [P, S2], U8)[:, :], sem(f"mask_in{i}")) for i in range(2))
            q_dram = [Slot(nc.dram_tensor(f"q_parts{b}", [D, 3, S], BF16).ap()) for b in range(B)]
            k_dram = [Slot(nc.dram_tensor(f"k_parts{b}", [D, 3, S2], BF16).ap()) for b in range(B)]

            s_bv = sem("bv_in")
            sync.dma_start(bv[:, :, :], a["bv"]).then_inc(s_bv, 16)
            sync.dma_start(bias_b[:, :], a["L1f_bias"]).then_inc(s_bv, 16)
            bv_in = (s_bv, 32)
            V.wait(bv_in)
            for n in norms.slots:
                t_z = v_(vector.memset(n.ap[:, :, 0:PAD], 0.0))
            t_v1 = v_(vector.memset(values.slots[0].ap, 1.0))
            V.wait(t_z, t_v1)

            def load_weights(slot, name, width, after):
                SP.wait(after)
                Progress.count += 1
                return slot.dma(sync.dma_start(slot.ap[:, 0:width], a[name]))

            def cut(src, part, t_src):
                V.wait(t_src, part.free)
                t = v_(vector.tensor_copy(part.ap[:, 0, :], src.ap))
                G.wait(t)
                t = g_(gpsimd.tensor_tensor(src.ap, src.ap, part.ap[:, 0, :], ALU.subtract))
                V.wait(t)
                t = v_(vector.tensor_copy(part.ap[:, 1, :], src.ap))
                G.wait(t)
                return g_(gpsimd.tensor_tensor(part.ap[:, 2, :], src.ap, part.ap[:, 1, :], ALU.subtract))

            def attention(b, L, w_in, done, mask=False):
                gi = int(L[1])
                wq = w_att.ap[:, 0:2 * D].rearrange("p (c n) -> p c n", c=C)
                wk = w_att.ap[:, 2 * D:4 * D].rearrange("p (c n) -> p c n", c=C)
                wv = w_att.ap[:, 4 * D:6 * D].rearrange("p (c n) -> p c n", c=C)
                wo = w_att.ap[:, 6 * D:10 * D].rearrange("p (g n) -> p g n", g=G4)
                yield from need((ctxs, 1), (norms, 1))
                cx, xn = ctxs.take(), norms.take()
                SP.wait(cx.free)
                for c in range(C):
                    cx_in = cx.dma(sync.dma_start(cx.ap[:, c, :], a["ctxT"][c * P:(c + 1) * P, b, :]))
                t_xn = yield from layer_norm(b, xn, works)
                PE.wait(w_in, cx_in, t_xn)

                def project(w, src, m, n0, bias, scale, dram, after_reads):
                    yield from need((banks, 1, 0), (works, 1), (parts, 1))
                    ps, f, part = banks.take(), works.take(), parts.take()
                    PE.wait(ps.free)
                    for c in range(C):
                        ins = tensor.matmul(ps.ap, w[:, c, m * P:(m + 1) * P], src[c], start=c == 0, stop=c == C - 1)
                    t = pe_(ins)
                    A.wait(t, f.free)
                    t = a_(scalar.activation(f.ap, ps.ap, ACT.Identity, bias=bias, scale=scale))
                    banks.give(ps, t)
                    yield
                    t = cut(f, part, t)
                    works.give(f, t)
                    SP.wait(t, after_reads)
                    mark = part.dma(sync.dma_start(dram.ap[m * P:(m + 1) * P, :, n0:n0 + S], part.ap))
                    parts.give(part, mark)
                    yield
                    return [mark]

                sent = []
                qd, kd = q_dram[b], k_dram[b]
                q_free, k_free = list(qd.free), list(kd.free)
                for m in range(C):
                    sent += yield from project(wq, [xn.ap[:, c, PAD:ROW] for c in range(C)], m, 0, sm(L + "_bq4", m), 0.25, qd, q_free)
                    for n in range(S2 // S):
                        sent += yield from project(wk, [cx.ap[:, c, n * S:(n + 1) * S] for c in range(C)], m, n * S,
                                                   vec(L + "_bk", m), 1.0, kd, k_free)
                norms.give(xn, (PE.sem, PE.n))
                yield from need((values, 1))
                va = values.take()
                for kt in range(0, KT, 2):
                    yield from need((banks, 1, 0))
                    ps = banks.take()
                    PE.wait(ps.free)
                    for k in range(2):
                        for c in range(C):
                            ins = tensor.matmul(ps.ap[:, k * D:(k + 1) * D], cx.ap[:, c, (kt + k) * P:(kt + k + 1) * P],
                                                wv[:, c, :], start=c == 0, stop=c == C - 1)
                    t = pe_(ins)
                    V.wait(t, va.free)
                    for k in range(2):
                        t_va = v_(vector.tensor_tensor(
                            va.ap[:, kt + k, :, 0:HD], ps.ap[:, k * D:(k + 1) * D].rearrange("p (h d) -> p h d", h=H),
                            bv[:, (0, 1, None, 2)[gi], :].rearrange("p (h d) -> p h d", h=H), ALU.add))
                    banks.give(ps, t_va)
                    yield
                ctxs.give(cx, (PE.sem, PE.n))

                if mask:
                    V.wait(masks.free)
                    for i in range(QT + KT // 2):
                        yield from need((mask_u8, 1))
                        mu = mask_u8.take()
                        SP.wait(mu.free)
                        if i < QT:
                            src, dst = a["mask"][b, i * P:(i + 1) * P, :], mu.ap
                        else:
                            k0 = 2 * (i - QT)
                            src = a["maskT"][b, k0 * P:(k0 + 2) * P, :].rearrange("(t p) q -> p t q", p=P)
                            dst = mu.ap.rearrange("p (t q) -> p t q", t=2)
                        t = mu.dma(sync.dma_start(dst, src))
                        V.wait(t)
                        t_mask = v_(vector.tensor_scalar(masks.ap[:, i * S2:(i + 1) * S2], mu.ap, -1.0, -MASKED, ALU.add, ALU.mult))
                        mask_u8.give(mu, t_mask)
                    PE.wait(t_mask)
                    yield

                yield from need((outs, 1))
                at = outs.take()
                group_reads = []
                for g in range(G4):
                    yield from need((stacks, 1), (maxes, 1), (shifts, 1))
                    st, mx, sh = stacks.take(), maxes.take(), shifts.take()
                    kst = st.ap[:, 0:2 * S2].bitcast(BF16).rearrange("p (h n) -> p h n", h=4)
                    qst = st.ap[:, 2 * S2:3 * S2].bitcast(BF16).rearrange("p (h n) -> p h n", h=4)
                    SP.wait(st.free, sent)
                    rows = slice(g * 4 * HD, (g + 1) * 4 * HD)
                    for i, (pq, pk) in enumerate(PAIRS):
                        sync.dma_start(qst[i * HD:(i + 1) * HD, :, :], qd.ap[rows, pq, :].rearrange("(h d) n -> d h n", d=HD)).then_inc(st.sem, 16)
                        sync.dma_start(kst[i * HD:(i + 1) * HD, :, :], kd.ap[rows, pk, :].rearrange("(h d) n -> d h n", d=HD)).then_inc(st.sem, 16)
                    sync.dma_start(kst[STACK:STACK + 2, :, :], a["ones"].rearrange("r (h n) -> r h n", h=4)).then_inc(st.sem, 16)
                    st.n += 16 * (2 * len(PAIRS) + 1)
                    st_in = (st.sem, st.n)
                    group_reads.append(st_in)
                    yield
                    V.wait(mx.free)
                    PE.wait(st_in)
                    for h in range(4):
                        for qt in range(QT):
                            yield from need((banks, 0, 1))
                            ps = banks.take(2)
                            PE.wait(ps.free)
                            for n in range(2):
                                ins = tensor.matmul(ps.ap[:, n, :], qst[0:STACK, h, qt * P:(qt + 1) * P], kst[0:STACK, h, n * S:(n + 1) * S],
                                                    start=True, stop=not mask)
                                if mask:
                                    ins = tensor.matmul(ps.ap[:, n, :], ident_b[:, :], masks.ap[:, qt * S2 + n * S:qt * S2 + (n + 1) * S],
                                                        start=False, stop=True)
                            t = pe_(ins)
                            V.wait(t)
                            t_mx = v_(vector.tensor_reduce(mx.ap[:, h * QT + qt:h * QT + qt + 1], ps.ap, AX.XY, ALU.max))
                            banks.give(ps, t_mx)
                            yield
                    if mask:
                        V.wait(t_mx)
                        t = v_(vector.tensor_scalar(mx.ap[:, 16:32], mx.ap[:, 0:16], 0.5 * MASKED, None, ALU.is_gt))
                        V.wait(t)
                        t = v_(vector.reciprocal(mx.ap[:, 16:32], mx.ap[:, 16:32]))
                        V.wait(t)
                        t = v_(vector.tensor_tensor(mx.ap[:, 32:48], mx.ap[:, 16:32], mx.ap[:, 16:32], ALU.subtract))
                        V.wait(t)
                        t_mx = v_(vector.tensor_tensor(mx.ap[:, 0:16], mx.ap[:, 0:16], mx.ap[:, 32:48], ALU.add))
                    yield from need((banks, 1, 0))
                    ps = banks.take()
                    PE.wait(t_mx, ps.free)
                    t = pe_(tensor.transpose(ps.ap[0:16, 0:P], mx.ap[:, 0:16], ident[:, :]))
                    V.wait(t, sh.free)
                    t = v_(vector.tensor_scalar(sh.ap[:, 0, :], ps.ap[0:16, 0:P], -1.0, None, ALU.mult))
                    V.wait(t)
                    t = v_(vector.scalar_tensor_tensor(out=sh.ap[:, 1, :], in0=ps.ap[0:16, 0:P], scalar=-1.0, in1=sh.ap[:, 0, :],
                                                       op0=ALU.mult, op1=ALU.subtract))
                    maxes.give(mx, t)
                    banks.give(ps, t)
                    SP.wait(t)
                    for i in range(2):
                        dst = qst[STACK + i:STACK + i + 1, :, :].rearrange("r h (t q) -> r (h t) q", q=P)
                        sync.dma_start(dst, sh.ap[:, i, :]).then_inc(sh.sem, 16)
                    sh.n += 32
                    sh_in = (sh.sem, sh.n)
                    shifts.give(sh, sh_in)
                    yield
                    yield from need((banks, 1, 0))
                    acc = banks.take()
                    waiting = []

                    def product(kt2, held):
                        for k in range(2):
                            for h in range(4):
                                kt = 2 * kt2 + k
                                ins = tensor.matmul(acc.ap[32 * h:32 * h + 32, :], va.ap[:, kt, 4 * g + h, :], held[h][0].ap[:, k, :],
                                                    start=kt == 0, stop=kt == KT - 1)
                        t = pe_(ins)
                        for p, _ in held:
                            probs.give(p, t)
                        return t

                    PE.wait(sh_in, t_va, acc.free)
                    for kt2 in range(KT // 2):
                        held = []
                        for h in range(4):
                            yield from need((banks, 0, 1), (probs, 1))
                            ps, pr = banks.take(2), probs.take()
                            PE.wait(ps.free)
                            for k in range(2):
                                kt = 2 * kt2 + k
                                ins = tensor.matmul(ps.ap[:, k, :], kst[0:STACK + 2, h, kt * P:(kt + 1) * P], qst[0:STACK + 2, h, :],
                                                    start=True, stop=not mask)
                                if mask:
                                    ins = tensor.matmul(ps.ap[:, k, :], ident_b[:, :], masks.ap[:, QT * S2 + kt * S:QT * S2 + (kt + 1) * S],
                                                        start=False, stop=True)
                            t = pe_(ins)
                            A.wait(t, pr.free)
                            t = a_(scalar.activation(pr.ap, ps.ap, ACT.Exp))
                            banks.give(ps, t)
                            held.append((pr, t))
                            if h == 1 and waiting:
                                PE.wait([m for _, m in waiting[0][1]])
                                product(*waiting.pop(0))
                            yield
                        waiting.append((kt2, held))
                    stacks.give(st, (PE.sem, PE.n))
                    PE.wait([m for _, m in waiting[0][1]])
                    t = product(*waiting.pop(0))
                    yield from need((works, 1))
                    w = works.take()
                    V.wait(t, w.free, at.free)
                    t = v_(vector.stream_shuffle(w.ap, acc.ap, [16 + i % 16 for i in range(32)]))
                    V.wait(t)
                    t = v_(vector.reciprocal(w.ap, w.ap))
                    V.wait(t)
                    t_at = v_(vector.tensor_tensor(at.ap[:, g, :], acc.ap, w.ap, ALU.mult))
                    works.give(w, t_at)
                    banks.give(acc, t_at)
                    yield
                values.give(va, (PE.sem, PE.n))
                if mask:
                    masks.free = [(PE.sem, PE.n)]
                qd.free = kd.free = group_reads
                PE.wait(t_at)
                for m in range(C):
                    yield from need((banks, 1, 0))
                    ps = banks.take()
                    PE.wait(ps.free)
                    for g in range(G4):
                        ins = tensor.matmul(ps.ap, wo[:, g, m * P:(m + 1) * P], at.ap[:, g, :], start=g == 0, stop=g == G4 - 1)
                    t = pe_(ins)
                    t = yield from gated_add(b, m, ps, t, gates[:, gi:gi + 1], sm(L + "_gbo", m))
                x_ready[b] = [t]
                outs.give(at, (PE.sem, PE.n))
                done.append((PE.sem, PE.n))

            def gated_add(b, m, ps, t, gate, gated_bias):
                yield from need((works, 1))
                w = works.take()
                A.wait(t, w.free)
                t = a_(scalar.activation(w.ap, ps.ap, ACT.Identity, bias=gated_bias, scale=gate))
                banks.give(ps, t)
                V.wait(t)
                t = v_(vector.tensor_tensor(tokens(b, m), tokens(b, m), w.ap, ALU.add))
                works.give(w, t)
                yield
                return t

            def binarize(w_in, done):
                halves = [(w_ff.ap[:, 0:FF0 * D].rearrange("p (c n) -> p c n", c=C), C, FF0 * P, 1.0),
                          (w_ff.ap[:, FF0 * D:2 * FF0 * D].rearrange("p (c n) -> p c n", c=FF0), FF0, D, D / (FF0 * P))]
                A.wait(w_in)
                V.wait(w_in)
                for w, nc_, width, extra in halves:
                    for n0 in range(0, width, 512):
                        n = min(512, width - n0)
                        yield from need((banks, 1, 0), (works, 2))
                        ps, ab, sg = banks.take(), works.take(), works.take()
                        PE.wait(ps.free)
                        t = None
                        for c in range(nc_):
                            A.wait(ab.free, t)
                            t = a_(scalar.activation(ab.ap[:, 0:n], w[:, c, n0:n0 + n], ACT.Abs))
                            PE.wait(t)
                            t = pe_(tensor.matmul(ps.ap[:, 0:n], ones_mean[:, :], ab.ap[:, 0:n], start=c == 0, stop=c == nc_ - 1))
                        A.wait(t)
                        t = a_(scalar.activation(ab.ap[:, 0:n], ps.ap[:, 0:n], ACT.Copy, scale=extra))
                        banks.give(ps, t)
                        V.wait(t)
                        for c in range(nc_):
                            A.wait(sg.free)
                            t = a_(scalar.activation(sg.ap[:, 0:n], w[:, c, n0:n0 + n], ACT.Sign))
                            V.wait(t)
                            t = v_(vector.tensor_tensor(sg.ap[:, 0:n], sg.ap[:, 0:n], ab.ap[:, 0:n], ALU.mult))
                            V.wait(t)
                            t = v_(vector.tensor_tensor(sg.ap[:, 0:n], sg.ap[:, 0:n], w[:, c, n0:n0 + n], ALU.subtract))
                            V.wait(t)
                            t = v_(vector.tensor_tensor(w[:, c, n0:n0 + n], w[:, c, n0:n0 + n], sg.ap[:, 0:n], ALU.add))
                            sg.free = [t]
                        works.give(ab, t)
                        works.give(sg, t)
                        yield
                done.append(t)

            def feed_forward0(b, w_ready, done):
                w1 = w_ff.ap[:, 0:FF0 * D].rearrange("p (c n) -> p c n", c=C)
                w2 = w_ff.ap[:, FF0 * D:2 * FF0 * D].rearrange("p (k n) -> p k n", k=FF0)
                yield from need((norms, 1))
                xn = norms.take()
                t_xn = yield from layer_norm(b, xn, works)
                while not w_ready:
                    yield
                yield from need((banks, 2, 0))
                acc = [banks.take() for _ in range(C)]
                PE.wait(w_ready, t_xn, acc[0].free, acc[1].free)
                before = None
                for i in range(FF0 + 1):
                    if i < FF0:
                        yield from need((banks, 1, 0), (works, 1))
                        ps, h = banks.take(), works.take()
                        PE.wait(ps.free)
                        for c in range(C):
                            ins = tensor.matmul(ps.ap, w1[:, c, i * P:(i + 1) * P], xn.ap[:, c, PAD:ROW], start=c == 0, stop=c == C - 1)
                        t = pe_(ins)
                        A.wait(t, h.free)
                        t_h = a_(scalar.activation(h.ap, ps.ap, ACT.Gelu, bias=vec("L0_b1", i)))
                        banks.give(ps, t_h)
                    if before is not None:
                        k, hb, t_hb = before
                        PE.wait(t_hb)
                        for m in range(C):
                            ins = tensor.matmul(acc[m].ap, w2[:, k, m * P:(m + 1) * P], hb.ap, start=k == 0, stop=k == FF0 - 1)
                        t = pe_(ins)
                        works.give(hb, t)
                    before = (i, h, t_h) if i < FF0 else None
                    yield
                norms.give(xn, (PE.sem, PE.n))
                t_acc = t
                for m in range(C):
                    t = yield from gated_add(b, m, acc[m], t_acc, gates[:, 4:5], sm("L0_gb2", m))
                x_ready[b] = [t]
                done.append((PE.sem, PE.n))

            def quantize(src, dst, inv, w):
                n = src.shape[-1]
                val, big, aux = (x.ap[:, 0:n] for x in w[:3])
                lo8, hi8 = w[3].ap.bitcast(FP8)[:, 0:n], w[3].ap.bitcast(FP8)[:, S:S + n]
                t = v_(vector.tensor_scalar(val, src, inv, None, ALU.mult))
                V.wait(t)
                v_(vector.tensor_scalar(lo8, val, 240.0, -240.0, ALU.min, ALU.max, saturate=False))
                t = v_(vector.tensor_scalar(aux, val, 0.5, 240.0, ALU.mult, ALU.min))
                V.wait(t)
                t = v_(vector.tensor_scalar(hi8, aux, -240.0, None, ALU.max, saturate=False))
                V.wait(t)
                t = v_(vector.scalar_tensor_tensor(out=big, in0=hi8, scalar=2.0, in1=lo8, op0=ALU.mult, op1=ALU.subtract))
                t = v_(vector.scalar_tensor_tensor(out=val, in0=val, scalar=-1.0, in1=val, op0=ALU.mult, op1=ALU.max))
                V.wait(t)
                t = v_(vector.scalar_tensor_tensor(out=big, in0=val, scalar=16.0, in1=big, op0=ALU.is_ge, op1=ALU.mult))
                t = v_(vector.tensor_scalar(val, val, 464.0, None, ALU.is_le))
                V.wait(t)
                t = v_(vector.reciprocal(aux, val))
                t2 = v_(vector.tensor_tensor(big, big, lo8, ALU.add))
                V.wait(t, t2)
                t = v_(vector.tensor_tensor(aux, aux, aux, ALU.subtract))
                V.wait(t)
                return v_(vector.tensor_tensor(dst, big, aux, ALU.add))

            def quantize_weights(done):
                yield from need((works, 4))
                w = [works.take() for _ in range(4)]
                s_k8 = sem("kernel_in")
                m = (s_k8, 16)
                SP.wait(*[x.free for x in w])
                sync.dma_start(w_ffb[:, :, :], a["L1f_w"]).then_inc(s_k8, 16)
                V.wait(m, *[x.free for x in w])
                flat = w_ffb[:, :, :].rearrange("p c n -> p (c n)")
                t = quantize(flat, flat, sm("inv_k"), w)
                for x in w:
                    works.give(x, t)
                yield
                done.append(t)

            def feed_forward1(b, w_ready, done):
                yield from need((norms, 1))
                xn = norms.take()
                t_xn = yield from layer_norm(b, xn, works)
                while not w_ready:
                    yield
                yield from need((works, 4), (parts, 1))
                w, part = [works.take() for _ in range(4)], parts.take()
                V.wait(t_xn, part.free, *[x.free for x in w])
                for c in range(C):
                    t = v_(vector.tensor_copy(part.ap[:, 2, :], xn.ap[:, c, PAD:ROW]))
                    V.wait(t)
                    t = quantize(part.ap[:, 2, :], part.ap[:, c, :], sm("inv_in"), w)
                    V.wait(t)
                    yield
                norms.give(xn, t)
                for x in w:
                    works.give(x, t)
                PE.wait(t, w_ready)
                for m in range(C):
                    yield from need((banks, 1, 0), (works, 1))
                    ps, y = banks.take(), works.take()
                    PE.wait(ps.free)
                    for c in range(C):
                        ins = tensor.matmul(ps.ap, w_ffb[:, c, m * P:(m + 1) * P], part.ap[:, c, :], start=c == 0, stop=c == C - 1)
                    t = pe_(ins)
                    yb = y.ap.bitcast(BF16)
                    V.wait(t, y.free)
                    t = v_(vector.tensor_scalar(yb[:, 0:S], ps.ap, sm("s_both"), None, ALU.mult))
                    banks.give(ps, t)
                    V.wait(t)
                    t = v_(vector.tensor_scalar(yb[:, S:2 * S], yb[:, 0:S], bias_b[:, m:m + 1], None, ALU.add))
                    V.wait(t)
                    t = v_(vector.scalar_tensor_tensor(out=tokens(b, m), in0=yb[:, S:2 * S], scalar=gates[:, 5:6], in1=tokens(b, m),
                                                       op0=ALU.mult, op1=ALU.add))
                    works.give(y, t)
                    yield
                parts.give(part, (PE.sem, PE.n))
                x_ready[b] = [t]
                done.append((PE.sem, PE.n))

            def attention_single(b, w_in, done):
                wt = w_att.ap[:, 0:2 * D].rearrange("p (c n) -> p c n", c=C)
                yield from need((ctxs, 1), (norms, 1), (stacks, 2))
                cx, xn, st, raw = ctxs.take(), norms.take(), stacks.take(), stacks.take()
                SP.wait(cx.free, raw.free)
                for c in range(C):
                    cx_in = cx.dma(sync.dma_start(cx.ap[:, c, :], a["ctxT"][c * P:(c + 1) * P, b, :]))
                ctok = raw.ap[:, 0:2 * S2].rearrange("p (t n) -> p t n", t=KT)
                ctok_in = raw.dma(sync.dma_start(ctok, a["ctx"][b].rearrange("(t p) n -> p t n", p=P)))
                t_xn = yield from layer_norm(b, xn, works)
                eo = st.ap[:, 0:2 * S2].rearrange("p (c n) -> p c n", c=C)
                ex = st.ap[:, 2 * S2:3 * S2].rearrange("p (c n) -> p c n", c=C)
                PE.wait(w_in, cx_in, t_xn)
                A.wait(st.free)
                for m in range(C):
                    for n in range(3):
                        yield from need((banks, 1, 0))
                        ps = banks.take()
                        PE.wait(ps.free)
                        for c in range(C):
                            src = xn.ap[:, c, PAD:ROW] if n == 2 else cx.ap[:, c, n * S:(n + 1) * S]
                            ins = tensor.matmul(ps.ap, wt[:, c, m * P:(m + 1) * P], src, start=c == 0, stop=c == C - 1)
                        t = pe_(ins)
                        A.wait(t)
                        dst = ex[:, m, :] if n == 2 else eo[:, m, n * S:(n + 1) * S]
                        t_e = a_(scalar.activation(dst, ps.ap, ACT.Identity, bias=vec("L2_b", m)))
                        banks.give(ps, t_e)
                        yield
                ctxs.give(cx, (PE.sem, PE.n))
                norms.give(xn, (PE.sem, PE.n))
                PE.wait(t_e, ctok_in)
                for qt in range(QT):
                    yield from need((banks, 0, 1), (probs, 2), (maxes, 1))
                    ps, pr, pt, mx = banks.take(2), probs.take(), probs.take(), maxes.take()
                    PE.wait(ps.free)
                    for n in range(2):
                        for c in range(C):
                            ins = tensor.matmul(ps.ap[:, n, :], ex[:, c, qt * P:(qt + 1) * P], eo[:, c, n * S:(n + 1) * S],
                                                start=c == 0, stop=c == C - 1)
                    t = pe_(ins)
                    V.wait(t, mx.free)
                    t = v_(vector.tensor_reduce(mx.ap[:, 0:1], ps.ap, AX.XY, ALU.max, negate=True))
                    yield
                    A.wait(t, pr.free)
                    t = a_(scalar.activation(pr.ap, ps.ap, ACT.Exp, bias=mx.ap[:, 0:1], accum_out=mx.ap[:, 1:2]))
                    banks.give(ps, t)
                    V.wait(t)
                    t = v_(vector.reciprocal(mx.ap[:, 2:3], mx.ap[:, 1:2]))
                    V.wait(t)
                    t_p = v_(vector.tensor_scalar(pr.ap, pr.ap, mx.ap[:, 2:3], None, ALU.mult))
                    maxes.give(mx, t_p)
                    yield
                    yield from need((banks, 0, 1))
                    ps = banks.take(2)
                    PE.wait(t_p, ps.free)
                    for kt in range(KT):
                        ins = tensor.transpose(ps.ap[:, kt // 4, (kt % 4) * P:(kt % 4 + 1) * P],
                                               pr.ap[:, kt // 4, (kt % 4) * P:(kt % 4 + 1) * P], ident[:, :])
                    t = pe_(ins)
                    probs.give(pr, t)
                    A.wait(t, pt.free)
                    t = a_(scalar.activation(pt.ap, ps.ap, ACT.Copy))
                    banks.give(ps, t)
                    yield
                    yield from need((banks, 1, 0))
                    ps = banks.take()
                    PE.wait(t, ps.free)
                    for m in range(C):
                        for kt in range(KT):
                            ins = tensor.matmul(ps.ap[:, m * P:(m + 1) * P], ctok[:, kt, m * P:(m + 1) * P],
                                                pt.ap[:, kt // 4, (kt % 4) * P:(kt % 4 + 1) * P], start=kt == 0, stop=kt == KT - 1)
                    t = pe_(ins)
                    probs.give(pt, t)
                    V.wait(t, t_xn)
                    for m in range(C):
                        xs = X[:, m, b, PAD + qt * P:PAD + (qt + 1) * P]
                        t_x = v_(vector.scalar_tensor_tensor(out=xs, in0=ps.ap[:, m * P:(m + 1) * P], scalar=gates[:, 2:3], in1=xs,
                                                             op0=ALU.mult, op1=ALU.add))
                    banks.give(ps, t_x)
                    yield
                stacks.give(st, (PE.sem, PE.n))
                stacks.give(raw, (PE.sem, PE.n))
                x_ready[b] = [t_x]
                done.append((PE.sem, PE.n))

            def feed_forward2(b, w_in, done):
                w3 = w_ff.ap[:, 0:6 * D].rearrange("p (w c n) -> p w c n", w=3, c=C)
                yield from need((norms, 1))
                xn = norms.take()
                t_xn = yield from layer_norm(b, xn, works)
                yield from need((outs, 1), (norms, 1))
                mixed, kact = outs.take(), norms.take()
                V.wait(t_xn, mixed.free, kact.free)
                for i, (mu, om) in enumerate((("mu_r", "om_r"), ("mu_k", "om_k"))):
                    for c in range(C):
                        dst = mixed.ap[:, 2 * i + c, :]
                        t = v_(vector.tensor_scalar(dst, xn.ap[:, c, PAD - 1:ROW - 1], sm(om, c), None, ALU.mult))
                        V.wait(t)
                        t = v_(vector.scalar_tensor_tensor(out=dst, in0=xn.ap[:, c, PAD:ROW], scalar=vec(mu, c), in1=dst,
                                                           op0=ALU.mult, op1=ALU.add))
                norms.give(xn, t)
                yield
                PE.wait(t, w_in)
                for m in range(C):
                    yield from need((banks, 1, 0))
                    ps = banks.take()
                    PE.wait(ps.free)
                    for c in range(C):
                        ins = tensor.matmul(ps.ap, w3[:, 1, c, m * P:(m + 1) * P], mixed.ap[:, 2 + c, :], start=c == 0, stop=c == C - 1)
                    t = pe_(ins)
                    V.wait(t)
                    t = v_(vector.tensor_scalar(kact.ap[:, m, PAD:ROW], ps.ap, 0.0, None, ALU.max))
                    banks.give(ps, t)
                    A.wait(t)
                    t_k = a_(scalar.activation(kact.ap[:, m, PAD:ROW], kact.ap[:, m, PAD:ROW], ACT.Square))
                    yield
                for m in range(C):
                    yield from need((banks, 2, 0), (works, 1))
                    pr, pk, sg = banks.take(), banks.take(), works.take()
                    PE.wait(pr.free, pk.free)
                    for c in range(C):
                        ins = tensor.matmul(pr.ap, w3[:, 0, c, m * P:(m + 1) * P], mixed.ap[:, c, :], start=c == 0, stop=c == C - 1)
                    t = pe_(ins)
                    V.wait(t, sg.free)
                    t = v_(vector.tensor_scalar(sg.ap, pr.ap, -80.0, None, ALU.max))
                    banks.give(pr, t)
                    A.wait(t)
                    t = a_(scalar.activation(sg.ap, sg.ap, ACT.Exp, scale=-1.0))
                    V.wait(t)
                    t = v_(vector.tensor_scalar(sg.ap, sg.ap, 1.0, None, ALU.add))
                    V.wait(t)
                    t_s = v_(vector.reciprocal(sg.ap, sg.ap))
                    PE.wait(t_k)
                    for c in range(C):
                        ins = tensor.matmul(pk.ap, w3[:, 2, c, m * P:(m + 1) * P], kact.ap[:, c, PAD:ROW], start=c == 0, stop=c == C - 1)
                    t = pe_(ins)
                    V.wait(t, t_s)
                    t = v_(vector.tensor_tensor(sg.ap, pk.ap, sg.ap, ALU.mult))
                    banks.give(pk, t)
                    V.wait(t)
                    t = v_(vector.scalar_tensor_tensor(out=tokens(b, m), in0=sg.ap, scalar=gates[:, 6:7], in1=tokens(b, m),
                                                       op0=ALU.mult, op1=ALU.add))
                    works.give(sg, t)
                    yield
                outs.give(mixed, (PE.sem, PE.n))
                norms.give(kact, (PE.sem, PE.n))
                x_ready[b] = [t]
                done.append((PE.sem, PE.n))

            def put_aside(b, done):
                yield from need((norms, 1))
                xn = norms.take()
                SP.wait(x_ready[b])
                s_keep = sem(f"kept{b}")
                for c in range(C):
                    sync.dma_start(x_kept[c * P:(c + 1) * P, b, :], tokens(b, c)).then_inc(s_keep, 16)
                kept[b] = (s_keep, 16 * C)
                t_xn = yield from layer_norm(b, xn, works)
                V.wait(t_xn, kept[b], (PE.sem, PE.n))
                for c in range(C):
                    t = v_(vector.tensor_copy(tokens(b, c), xn.ap[:, c, PAD:ROW]))
                norms.give(xn, t)
                x_ready[b] = [t]
                done.append(t)
                yield

            def loader(slot, name, width, users, box):
                while len(users) < (B if users is not NONE else 0):
                    yield
                box.append(load_weights(slot, name, width, list(users)))

            NONE = []
            jobs, turn, layer_no = [], [0] * B, [0]

            def layer(name, job, slot, wname, width, before, prepare=None):
                box, ready, done = [], [], []
                if wname:
                    jobs.append(loader(slot, wname, width, before, box))
                if prepare:
                    jobs.append(prepare(box, ready))
                layer_no[0] += 1
                for b in range(B):
                    jobs.append(in_turn(b, layer_no[0], job(b, box, ready, done)))
                return done

            def in_turn(b, number, job):
                while turn[b] != number - 1:
                    yield
                yield from job
                turn[b] = number

            def wait_box(box):
                while not box:
                    yield

            def with_box(fn):
                def job(b, box, ready, done):
                    def late():
                        yield from wait_box(box)
                        yield from fn(b, box[0], done)
                    return late()
                return job

            def prep(fn):
                def job(box, ready):
                    def late():
                        yield from wait_box(box)
                        yield from fn(box[0], ready)
                    return late()
                return job

            A.wait(t_gate)
            V.wait(t_gate)
            users_att, users_ff = NONE, NONE
            if stages >= 1:
                users_att = layer("L0x", with_box(lambda b, m, d: attention(b, "L0", m, d)), w_att, "L0_att", 10 * D, users_att)
            if stages >= 2:
                users_ff = layer("L0f", lambda b, box, ready, d: feed_forward0(b, ready, d), w_ff, "L0_ff", 2 * FF0 * D, users_ff,
                                 prep(binarize))
            if stages >= 3:
                users_att = layer("L1x", with_box(lambda b, m, d: attention(b, "L1", m, d, mask=True)), w_att, "L1_att", 10 * D, users_att)
            if stages >= 4:
                layer("L1f", lambda b, box, ready, d: feed_forward1(b, ready, d), None, None, 0, None,
                      lambda box, ready: quantize_weights(ready))
            if stages >= 5:
                users_att = layer("L2x", with_box(lambda b, m, d: attention_single(b, m, d)), w_att, "L2_att", 2 * D, users_att)
            if stages >= 6:
                users_ff = layer("L2f", with_box(lambda b, m, d: feed_forward2(b, m, d)), w_ff, "L2_ff", 6 * D, users_ff)
            if stages >= 7:
                users_att = layer("L3x", with_box(lambda b, m, d: attention(b, "L3", m, d)), w_att, "L3_att", 10 * D, users_att)
            if stages >= 8:
                layer("norm", lambda b, box, ready, d: put_aside(b, d), None, None, 0, None)
            run_jobs(jobs, 3)
            SP.wait(*[(s.sem, s.n) for s in parts.slots])

        with ExitStack() as p1:
            first_part(p1)

        def last_part(p2):
            def psb(name, shape, dt=F32):
                return sb(name, shape, dt, p2)

            every = [(q.sem, q.n) for q in (PE, V, A, G)]
            for q in (PE, V, A, G, SP):
                q.wait(*every)

            QW = C * 3 * 4 * LHD + 2 * D
            FW = C * 2 * HT * P + HT * D
            xs_hi, xs_lo = psb("xs_hi", [P, C, B, S], F32R), psb("xs_lo", [P, C, B, S], F32R)
            quads = Ring(Slot((psb(f"quad_hi{i}", [P, QW], F32R), psb(f"quad_lo{i}", [P, QW], F32R))) for i in range(2))
            w12 = Slot((psb("w12_hi", [P, FW], F32R), psb("w12_lo", [P, FW], F32R)))
            staged = Ring(Slot(psb(f"staged{i}", [P, 1024])[:, :], sem(f"staged_in{i}")) for i in range(2))
            base = psb("rotary_base", [P, 2, QT, 2, LHD])
            rot = Slot(psb("rotary", [P, 2, QT, 2, LHD])[:, :, :, :, :])
            scales = Slot(psb("qk_scales", [P, 2, LHD])[:, :, :], sem("scales_in"))
            band = psb("band_bias", [P, 2 * P], BF16)
            keys = Ring(Slot(psb(f"keys{i}", [P, C, ROW])[:, :, :]) for i in range(2))
            vals = Ring(Slot(psb(f"vals{i}", [P, QT, 4 * LHD])[:, :, :]) for i in range(2))
            queries = Ring(Slot(psb(f"queries{i}", [P, 4, P])[:, :, :]) for i in range(3))
            pairs = Ring(Slot((psb(f"pair_hi{i}", [P, C, S], F32R), psb(f"pair_lo{i}", [P, C, S], F32R))) for i in range(2))
            hids = Ring(Slot((psb(f"hid_hi{i}", [P, S], F32R), psb(f"hid_lo{i}", [P, S], F32R))) for i in range(2))
            probs = Ring(Slot(psb(f"lprobs{i}", [P, 4, 2 * P])[:, :, :]) for i in range(2))
            works = Ring(Slot(psb(f"lwork{i}", [P, S])[:, :]) for i in range(6))
            stats = Ring(Slot(psb(f"stat{i}", [P, 32])[:, :]) for i in range(8))

            s_c2 = sem("constants_in")
            sync.dma_start(base[:, :, :, :, :], a["rotary"]).then_inc(s_c2, 16)
            sync.dma_start(band[:, :], a["band"]).then_inc(s_c2, 16)
            c2_in = (s_c2, 32)
            PE.wait(c2_in)
            V.wait(c2_in)
            for q_ in queries.slots:
                for h in range(4):
                    lo = 64 * (1 - h % 2)
                    t = v_(vector.memset(q_.ap[lo:lo + 64, h, :], 0.0))
            for p_ in probs.slots:
                t = v_(vector.memset(p_.ap[:, :, 0:64], 0.0))
            PE.wait(t)
            V.wait(t)
            G.wait(t)

            def split3(ps, wh, wl, xh, xl, start, stop, w_moves=False):
                order = [(wh, xh), (wh, xl), (wl, xh)] if not w_moves else [(xh, wh), (xh, wl), (xl, wh)]
                for n, (l, r) in enumerate(order):
                    ins = tensor.matmul(ps, l, r, start=start and n == 0, stop=stop and n == 2)
                return ins

            def load_split(dst, src, width, after, box):
                hi, lo = dst
                for n0 in range(0, width, 1024):
                    n = min(1024, width - n0)
                    yield from need((staged, 1))
                    s = staged.take()
                    SP.wait(s.free)
                    t = s.dma(sync.dma_start(s.ap[:, 0:n], src[:, n0:n0 + n]))
                    V.wait(t, after)
                    t = v_(vector.tensor_copy(hi[:, n0:n0 + n], s.ap[:, 0:n]))
                    G.wait(t)
                    t = g_(gpsimd.tensor_tensor(lo[:, n0:n0 + n], s.ap[:, 0:n], hi[:, n0:n0 + n].bitcast(F32), ALU.subtract))
                    staged.give(s, t)
                    yield
                box.append(t)

            xs_mark = [None] * B
            xs_read = [[] for _ in range(B)]

            def split_tokens(b):
                V.wait(x_ready[b], xs_read[b])
                for c in range(C):
                    t = v_(vector.tensor_copy(xs_hi[:, c, b, :], tokens(b, c, c)))
                G.wait(t, x_ready[b])
                for c in range(C):
                    t = g_(gpsimd.tensor_tensor(xs_lo[:, c, b, :], tokens(b, c, c), xs_hi[:, c, b, :].bitcast(F32), ALU.subtract))
                xs_mark[b] = t

            def rotary_tables(d, after, box):
                SP.wait(scales.free)
                t = scales.dma(sync.dma_start(scales.ap, a["qk_scale"][d]))
                V.wait(t, after)
                h = LHD // 2
                v_(vector.tensor_tensor(rot.ap[:, 0], base[:, 0], bc(scales.ap, 1, QT), ALU.mult))
                v_(vector.tensor_tensor(rot.ap[:, 1, :, :, 0:h], base[:, 1, :, :, 0:h], bc(scales.ap[:, :, h:LHD], 1, QT), ALU.mult))
                t = v_(vector.tensor_tensor(rot.ap[:, 1, :, :, h:LHD], base[:, 1, :, :, h:LHD], bc(scales.ap[:, :, 0:h], 1, QT), ALU.mult))
                scales.free = [t]
                box.append(t)
                yield

            def attend(d, b, w, w_in, rot_in, done):
                wh, wl = w
                cols = 3 * 4 * LHD
                W = lambda w_, c, lo, hi: w_[:, c * cols + lo:c * cols + hi]
                yield from need((keys, 1), (vals, 1), (pairs, 1))
                kT, va, att = keys.take(), vals.take(), pairs.take()
                for tt in range(QT):
                    yield from need((banks, 2, 0), (works, 4), (stats, 1), (queries, 1))
                    qk, vp = banks.take(), banks.take()
                    st = stats.take()
                    PE.wait(w_in, xs_mark[b], qk.free, vp.free)
                    for c in range(C):
                        tok = slice(tt * P, (tt + 1) * P)
                        for x_, w_, n in ((xs_hi, wh, 0), (xs_hi, wl, 1), (xs_lo, wh, 2)):
                            first, last = c == 0 and n == 0, c == C - 1 and n == 2
                            ins = tensor.matmul(qk.ap, x_[:, c, b, tok], W(w_, c, 0, 512), start=first, stop=last)
                            ins = tensor.matmul(vp.ap[:, 0:256], x_[:, c, b, tok], W(w_, c, 512, 768), start=first, stop=last)
                    t = pe_(ins)
                    sq, qn, t1, t2 = (works.take() for _ in range(4))
                    A.wait(t, va.free, sq.free)
                    t_sq = a_(scalar.activation(sq.ap, qk.ap, ACT.Square))
                    t_v = a_(scalar.activation(va.ap[:, tt, :], vp.ap[:, 0:256], ACT.Copy))
                    banks.give(vp, t_v)
                    yield
                    ss, y, tmp = st.ap[:, 0:8], st.ap[:, 8:16], st.ap[:, 16:24]
                    V.wait(t_sq, st.free)
                    m = v_(vector.tensor_reduce(ss, sq.ap.rearrange("p (h d) -> p h d", d=LHD), AX.X, ALU.add))
                    works.give(sq, m)
                    V.wait(m)
                    m = v_(vector.tensor_scalar(ss, ss, 1e-24, None, ALU.max))
                    A.wait(m)
                    m2 = a_(scalar.activation(y, ss, ACT.Ln, scale=float(2 ** 20)))
                    A.wait(m2)
                    m2 = a_(scalar.activation(y, y, ACT.Exp, scale=-0.5, bias=eps_col[:, 1:2]))
                    yield
                    V.wait(m2)
                    m = rsqrt_newton(y, lambda o, i: vector.tensor_tensor(o, ss, i, ALU.mult), y, tmp)
                    V.wait(m, qn.free)
                    t_qn = v_(vector.tensor_tensor(qn.ap.rearrange("p (h d) -> p h d", d=LHD), qk.ap.rearrange("p (h d) -> p h d", d=LHD),
                                                   bc(y, 2, LHD), ALU.mult))
                    banks.give(qk, t_qn)
                    stats.give(st, t_qn)
                    v4 = lambda x, lo=0, hi=LHD: x.rearrange("p (s h d) -> p s h d", s=2, d=LHD)[:, :, :, lo:hi]
                    hd2 = LHD // 2
                    G.wait(t_qn, t1.free, rot_in)
                    t_t1 = g_(gpsimd.tensor_tensor(v4(t1.ap), v4(qn.ap), bc(rot.ap[:, 0, tt], 2, 4), ALU.mult))
                    V.wait(t_qn, t2.free, rot_in)
                    v_(vector.tensor_tensor(v4(t2.ap, 0, hd2), v4(qn.ap, hd2, LHD), bc(rot.ap[:, 1, tt, :, 0:hd2], 2, 4), ALU.mult))
                    t_t2 = v_(vector.tensor_tensor(v4(t2.ap, hd2, LHD), v4(qn.ap, 0, hd2), bc(rot.ap[:, 1, tt, :, hd2:LHD], 2, 4), ALU.mult))
                    works.give(qn, t_t1, t_t2)
                    G.wait(t_t1, t_t2)
                    t_r = g_(gpsimd.tensor_tensor(t1.ap, t1.ap, t2.ap, ALU.add))
                    works.give(t2, t_r)
                    yield
                    yield from need((banks, 1, 0), (queries, 1))
                    ps, qz = banks.take(), queries.take()
                    PE.wait(t_r, ps.free)
                    for j in range(4):
                        ins = tensor.transpose(ps.ap[:, j * P:(j + 1) * P], t1.ap[:, j * P:(j + 1) * P], ident[:, :])
                    t = pe_(ins)
                    works.give(t1, t)
                    A.wait(t, kT.free)
                    t_k = a_(scalar.activation(kT.ap[:, :, PAD + tt * P:PAD + (tt + 1) * P], ps.ap[:, 2 * P:4 * P].rearrange("p (j n) -> p j n", j=2), ACT.Copy))
                    V.wait(t_k, qz.free)
                    for e in range(2):
                        r = slice(64 * e, 64 * e + 64)
                        t_q = v_(vector.tensor_copy(qz.ap[r, e:4:2, :], ps.ap[r, 0:2 * P].rearrange("p (j n) -> p j n", j=2)))
                    banks.give(ps, t_k, t_q)
                    yield
                    yield from need((banks, 0, 1), (probs, 1), (stats, 1))
                    ps, pr, st = banks.take(2), probs.take(), stats.take()
                    f = 64 if tt else P
                    PE.wait(t_k, t_q, ps.free)
                    for h in range(4):
                        o = ps.ap[:, h // 2, (h % 2) * 256 + f:(h % 2) * 256 + 256]
                        tensor.matmul(o, qz.ap[:, h, :], kT.ap[:, h // 2, PAD + (tt - 1) * P + f:PAD + (tt + 1) * P], start=True, stop=False)
                        ins = tensor.matmul(o, ident_b[:, :], band[:, f:256], start=False, stop=True)
                    t = pe_(ins)
                    queries.give(qz, t)
                    sc = ps.ap.rearrange("p b (h n) -> p (b h) n", h=2)
                    V.wait(t, st.free)
                    t = v_(vector.tensor_reduce(st.ap[:, 0:4], sc[:, :, f:256], AX.X, ALU.max, negate=True))
                    A.wait(t, pr.free)
                    yield
                    for h in range(4):
                        t = a_(scalar.activation(pr.ap[:, h, f:256], sc[:, h, f:256], ACT.Exp, bias=st.ap[:, h:h + 1], accum_out=st.ap[:, 4 + h:5 + h]))
                    banks.give(ps, t)
                    V.wait(t)
                    t = v_(vector.reciprocal(st.ap[:, 8:12], st.ap[:, 4:8]))
                    G.wait(t)
                    t_p = g_(gpsimd.tensor_tensor(pr.ap[:, :, f:256], pr.ap[:, :, f:256], bc(st.ap[:, 8:12], 2, 256 - f), ALU.mult))
                    stats.give(st, t_p)
                    yield
                    yield from need((banks, 2, 0), (works, 1))
                    acc = banks.take()
                    js = (0, 1) if tt else (1,)
                    PE.wait(t_p, t_v, acc.free)
                    for pair in range(2):
                        yield from need((banks, 1, 0), (works, 1))
                        ps, pt = banks.take(), works.take()
                        PE.wait(ps.free)
                        for hh in range(2):
                            for j in js:
                                n0 = (2 * hh + j) * P
                                ins = tensor.transpose(ps.ap[:, n0:n0 + P], pr.ap[:, 2 * pair + hh, j * P:(j + 1) * P], ident[:, :])
                        t = pe_(ins)
                        v2_ = lambda x: x.rearrange("p (h n) -> p h n", h=2)[:, :, js[0] * P:2 * P]
                        if pair == 0:
                            A.wait(t, pt.free)
                            t = a_(scalar.activation(v2_(pt.ap), v2_(ps.ap), ACT.Copy))
                        else:
                            V.wait(t, pt.free)
                            t = v_(vector.tensor_copy(v2_(pt.ap), v2_(ps.ap)))
                        banks.give(ps, t)
                        yield
                        PE.wait(t)
                        for j in js:
                            for hh in range(2):
                                hd = (2 * pair + hh) * LHD
                                n0 = (2 * hh + j) * P
                                ins = tensor.matmul(acc.ap[64 * hh:64 * hh + 64, pair * P:(pair + 1) * P], va.ap[:, tt - 1 + j, hd:hd + LHD],
                                                    pt.ap[:, n0:n0 + P], start=j == js[0], stop=j == 1)
                        t = pe_(ins)
                        works.give(pt, t)
                    probs.give(pr, t)
                    hi, lo = att.ap
                    o2 = acc.ap[:, 0:2 * P].rearrange("p (j n) -> p j n", j=2)
                    tok = slice(tt * P, (tt + 1) * P)
                    A.wait(t, att.free)
                    t = a_(scalar.activation(hi[:, :, tok], o2, ACT.Copy))
                    V.wait(t, att.free)
                    t_o = v_(vector.tensor_tensor(lo[:, :, tok], o2, hi[:, :, tok].bitcast(F32), ALU.subtract))
                    banks.give(acc, t_o)
                    yield
                xs_read[b].append((PE.sem, PE.n))
                keys.give(kT, (PE.sem, PE.n))
                vals.give(va, (PE.sem, PE.n))
                PE.wait(t_o)
                for m in range(C):
                    yield from need((banks, 1, 0))
                    ps = banks.take()
                    PE.wait(ps.free)
                    for k in range(2):
                        at_ = C * cols + k * D + m * P
                        ins = split3(ps.ap, wh[:, at_:at_ + P], wl[:, at_:at_ + P], hi[:, k, :], lo[:, k, :], k == 0, k == 1)
                    t = pe_(ins)
                    V.wait(t, x_ready[b], xs_mark[b])
                    t = v_(vector.tensor_tensor(tokens(b, m), ps.ap, tokens(b, m), ALU.add))
                    banks.give(ps, t)
                    yield
                x_ready[b] = [t]
                pairs.give(att, (PE.sem, PE.n))
                done.append((PE.sem, PE.n))

            def feed_forward3(d, b, w_in, done):
                wh, wl = w12.ap
                yield from need((keys, 1), (pairs, 1))
                xc, xn = keys.take(), pairs.take()
                rstd, t_rs = yield from centred_rstd(b, 1, xc, works)
                hi, lo = xn.ap
                V.wait(t_rs)
                for c in range(C):
                    t = v_(vector.scalar_tensor_tensor(out=xc.ap[:, c, PAD:ROW], in0=xc.ap[:, c, PAD:ROW], scalar=vec(f"ln_g{d}", c),
                                                       in1=rstd.ap, op0=ALU.mult, op1=ALU.mult))
                works.give(rstd, t)
                A.wait(t, xn.free)
                V.wait(t, xn.free)
                for c in range(C):
                    t = a_(scalar.activation(hi[:, c, :], xc.ap[:, c, PAD:ROW], ACT.Identity, bias=vec(f"ln_b{d}", c)))
                    V.wait(t)
                    t_xn = v_(vector.scalar_tensor_tensor(out=lo[:, c, :], in0=xc.ap[:, c, PAD:ROW], scalar=vec(f"ln_b{d}", c),
                                                          in1=hi[:, c, :].bitcast(F32), op0=ALU.add, op1=ALU.subtract))
                keys.give(xc, t_xn)
                yield
                yield from need((banks, 2, 0))
                acc = [banks.take() for _ in range(C)]
                PE.wait(w_in, t_xn, acc[0].free, acc[1].free)
                before = None
                for i in range(HT + 1):
                    if i < HT:
                        yield from need((banks, 2, 0), (works, 2))
                        pa, pg, g, h = banks.take(), banks.take(), works.take(), works.take()
                        PE.wait(pa.free, pg.free)
                        for ps, k in ((pg, 2 * i + 1), (pa, 2 * i)):
                            for c in range(C):
                                at_ = c * 2 * HT * P + k * P
                                ins = split3(ps.ap, wh[:, at_:at_ + P], wl[:, at_:at_ + P], hi[:, c, :], lo[:, c, :], c == 0, c == C - 1)
                            t = pe_(ins)
                            if ps is pg:
                                A.wait(t, g.free)
                                t_g = a_(scalar.activation(g.ap, pg.ap, ACT.Gelu, bias=vec(f"b1g{d}", i)))
                                banks.give(pg, t_g)
                        V.wait(t, t_g, h.free)
                        t = v_(vector.scalar_tensor_tensor(out=h.ap, in0=pa.ap, scalar=vec(f"b1a{d}", i), in1=g.ap, op0=ALU.add, op1=ALU.mult))
                        banks.give(pa, t)
                        works.give(g, t)
                        t_gated = t
                    if before is not None:
                        k, hb, t_hb = before
                        PE.wait(t_hb)
                        for m in range(C):
                            at_ = C * 2 * HT * P + k * D + m * P
                            ins = split3(acc[m].ap, wh[:, at_:at_ + P], wl[:, at_:at_ + P], hb.ap[0][:, :], hb.ap[1][:, :], k == 0, k == HT - 1)
                        t = pe_(ins)
                        hids.give(hb, t)
                    if i < HT:
                        yield from need((hids, 1))
                        hid = hids.take()
                        V.wait(t_gated, hid.free)
                        t_hi = v_(vector.tensor_copy(hid.ap[0][:, :], h.ap))
                        G.wait(t_hi)
                        t_h = g_(gpsimd.tensor_tensor(hid.ap[1][:, :], h.ap, hid.ap[0][:, :].bitcast(F32), ALU.subtract))
                        works.give(h, t_h)
                        before = (i, hid, t_h)
                    yield
                pairs.give(xn, (PE.sem, PE.n))
                V.wait(t)
                for m in range(C):
                    t_x = v_(vector.scalar_tensor_tensor(out=tokens(b, m), in0=acc[m].ap, scalar=vec(f"b2{d}", m), in1=tokens(b, m),
                                                         op0=ALU.add, op1=ALU.add))
                    banks.give(acc[m], t_x)
                x_ready[b] = [t_x]
                xs_read[b] = xs_read[b][-4:]
                if d < depths - 1:
                    split_tokens(b)
                    xs_read[b] = []
                done.append((PE.sem, PE.n))
                yield

            for b in range(B):
                split_tokens(b)

            jobs, turn, n_layer = [], [0] * B, 0

            def in_turn(b, number, job):
                while turn[b] != number - 1:
                    yield
                yield from job
                turn[b] = number

            def filled(box):
                while not box:
                    yield

            quad_in, rot_box, ff_in, used_ff, used_quads = {}, {}, {}, {-1: []}, {}

            def load_quad(d, g):
                yield from need((quads, 1))
                q_ = quads.take()
                box = []
                yield from load_split(q_.ap, a["quads"][d, g], QW, q_.free, box)
                quad_in[d, g] = (q_, box[0])

            def load_ff(d):
                while d and len(used_ff[d - 1]) < B:
                    yield
                box = []
                yield from load_split(w12.ap, a["w12"][d], FW, used_ff[d - 1], box)
                ff_in[d] = box[0]

            def make_tables(d):
                while d and len(used_quads[d - 1, 3]) < B:
                    yield
                box = []
                after = used_quads[d - 1, 3] if d else []
                yield from rotary_tables(d, after + [(G.sem, G.n)], box)
                rot_box[d] = box[0]

            def unit(d, g, b):
                while (d, g) not in quad_in or d not in rot_box:
                    yield
                q_, w_in = quad_in[d, g]
                yield from attend(d, b, q_.ap, w_in, rot_box[d], used_quads[d, g])
                if len(used_quads[d, g]) == B:
                    quads.give(q_, *used_quads[d, g])

            def ff(d, b):
                while d not in ff_in:
                    yield
                yield from feed_forward3(d, b, ff_in[d], used_ff[d])

            for d in range(depths):
                used_ff[d] = []
                for g in range(4):
                    used_quads[d, g] = []
                if d == 0:
                    jobs += [load_quad(0, 0), make_tables(0)]
                for g in range(4):
                    n_layer += 1
                    for b in range(B):
                        if b == 2:
                            jobs.append(load_quad(d, g + 1) if g < 3 else load_ff(d))
                        jobs.append(in_turn(b, n_layer, unit(d, g, b)))
                n_layer += 1
                for b in range(B):
                    if b == 1 and d < depths - 1:
                        jobs += [make_tables(d + 1), load_quad(d + 1, 0)]
                    jobs.append(in_turn(b, n_layer, ff(d, b)))
            run_jobs(jobs, 3)

        if stages >= 8:
            with ExitStack() as p2:
                last_part(p2)

        s_out = sem("out_written")
        with ExitStack() as p3:
            if stages >= 8:
                V.wait((PE.sem, PE.n), (A.sem, A.n), (G.sem, G.n), (V.sem, V.n))
                SP.wait((PE.sem, PE.n), (A.sem, A.n), (G.sem, G.n), (V.sem, V.n), *kept)
                back = sb("x_back", [P, C, B, S], F32, p3)
            for b in range(B):
                t = x_ready[b]
                if stages >= 8:
                    s_back = sem(f"back{b}")
                    for c in range(C):
                        sync.dma_start(back[:, c, b, :], x_kept[c * P:(c + 1) * P, b, :]).then_inc(s_back, 16)
                    V.wait(x_ready[b], (s_back, 16 * C))
                    for c in range(C):
                        t = v_(vector.scalar_tensor_tensor(out=back[:, c, b, :], in0=tokens(b, c), scalar=gates[:, 7:8],
                                                           in1=back[:, c, b, :], op0=ALU.mult, op1=ALU.add))
                SP.wait(t)
                for c in range(C):
                    src = back[:, c, b, :] if stages >= 8 else tokens(b, c)
                    sync.dma_start(out[c * P:(c + 1) * P, b, :], src).then_inc(s_out, 16)
        sync.wait_ge(s_out, 16 * C * B)


def _layout(x):
    n = x.shape[0] // P
    return np.ascontiguousarray(x.reshape(n, P, -1).transpose(1, 0, 2).reshape(P, -1))


def lay_out(i):
    i = {k: np.asarray(v) for k, v in i.items()}
    col = lambda v: np.ascontiguousarray(v.reshape(-1, P).T)
    rep = lambda v: np.broadcast_to(v.reshape(1, -1), (P, v.size))
    a = {}
    a["xT"] = np.ascontiguousarray(i["x"].transpose(2, 0, 1))
    a["ctxT"] = np.ascontiguousarray(i["ctx_1024"].transpose(2, 0, 1))
    a["ctx"] = np.ascontiguousarray(i["ctx_1024"])
    m = i["mask_BxSxS2_bf1"]
    a["mask"] = np.ascontiguousarray(m).view(np.uint8)
    a["maskT"] = np.ascontiguousarray(m.transpose(0, 2, 1)).view(np.uint8)

    def att(L, wq, wk, wv, wo):
        wop = np.zeros((H, 32, D), np.float32)
        wop[:, :HD] = wo.reshape(H, HD, D)
        a[L] = np.ascontiguousarray(np.concatenate([_layout(wq), _layout(wk), _layout(wv), _layout(wop.reshape(H * 32, D))], 1))

    flat = lambda w: w.transpose(1, 0, 2).reshape(D, D)
    att("L0_att", *(i[f"L0_xattn_w{n}"].T for n in "qkvo"))
    att("L1_att", *(flat(i[f"L1_xattn_W{n}"]) for n in "qkv"), i["L1_xattn_Wo"])
    att("L3_att", *(i[f"L3_xattn_W{n}"].T for n in "qkvo"))
    a["L0_ff"] = np.ascontiguousarray(np.concatenate([_layout(i["L0_ffn_w1"].T), _layout(i["L0_ffn_w2"].T)], 1))
    a["L1f_w"] = _layout(i["L1_ffn_kernel"]).reshape(P, C, D)
    a["L1f_bias"] = col(i["L1_ffn_bias"])
    a["L2_att"] = _layout(i["L2_xattn_W"].T)
    a["L2_ff"] = np.ascontiguousarray(np.concatenate([_layout(i[f"L2_ffn_W_{n}"].T) for n in "rkv"], 1))
    a["bv"] = np.ascontiguousarray(np.stack([rep(i[f"{L}_xattn_bv"]) for L in ("L0", "L1", "L3")], 1))
    cols = {
        "L0_b1": col(i["L0_ffn_b1"]), "L0_b2": col(i["L0_ffn_b2"]), "L2_b": col(i["L2_xattn_b"]),
        "mu_r": col(i["L2_ffn_mu_r"]), "mu_k": col(i["L2_ffn_mu_k"]),
        "g_x": rep(i["g_xattn"]), "g_f": rep(i["g_ffn"]),
        "s_in": rep(i["L1_ffn_input_scale"]), "s_k": rep(i["L1_ffn_kernel_scale"]),
    }
    for L in ("L0", "L1", "L3"):
        for n in "qko":
            cols[f"{L}_b{n}"] = col(i[f"{L}_xattn_b{n}"])
    pad = lambda v: np.concatenate([v, np.zeros(HT * P - HID, np.float32)])
    for d in range(DEPTH):
        cols[f"ln_g{d}"], cols[f"ln_b{d}"] = col(i["L3_ffn_ln_g"][d]), col(i["L3_ffn_ln_b"][d])
        cols[f"b1a{d}"], cols[f"b1g{d}"] = col(pad(i["L3_ffn_b1"][d][:HID])), col(pad(i["L3_ffn_b1"][d][HID:]))
        cols[f"b2{d}"] = col(i["L3_ffn_b2"][d])
    a["vecs"] = np.zeros((P, N_VECS), np.float32)
    for name, at in VECS.items():
        a["vecs"][:, at:at + cols[name].shape[1]] = cols[name]
    a["ident"] = np.eye(P, dtype=np.float32)
    bf16 = i["L1_ffn_kernel"].dtype
    a["ones"] = np.ones((2, 4 * S2), bf16)
    n, h = S, LHD // 2
    half = np.arange(0, LHD, 2, dtype=np.float32)
    t = np.arange(n, dtype=np.float32)
    freqs = t[:, None] * (1.0 / 10000.0 ** (half / LHD)).astype(np.float32)[None]
    power = (t - n // 2) / (WIN // 2)
    scale = ((half + 0.4 * LHD) / (1.4 * LHD)).astype(np.float32)[None] ** power[:, None]
    cos, sin = np.cos(freqs), np.sin(freqs)
    tab = np.zeros((2, n, 2, LHD), np.float32)
    for j, f in enumerate((8.0 * scale, 1.0 / scale)):
        tab[0, :, j] = np.concatenate([cos * f, cos * f], 1)
        tab[1, :, j] = np.concatenate([-sin * f, sin * f], 1)
    a["rotary"] = np.ascontiguousarray(tab.reshape(2, QT, P, 2, LHD).transpose(2, 0, 1, 3, 4))
    back = np.arange(P)[:, None] - (np.arange(2 * P)[None] - P)
    a["band"] = np.where((back >= 0) & (back <= WIN), 0.0, MASKED).astype(bf16)
    qs = np.stack([i["L3_ffn_q_scale"], i["L3_ffn_k_scale"]], 1)
    a["qk_scale"] = np.ascontiguousarray(np.broadcast_to(qs[:, None], (DEPTH, P, 2, LHD)))
    wqkv = i["L3_ffn_Wqkv"].reshape(DEPTH, D, 3, 4, 4 * LHD).transpose(0, 3, 1, 2, 4).reshape(DEPTH, 4, D, 12 * LHD)
    wo = i["L3_ffn_Wo"].reshape(DEPTH, 4, 4 * LHD, D)
    a["quads"] = np.stack([np.stack([np.concatenate([_layout(wqkv[d, g]), _layout(wo[d, g])], 1) for g in range(4)]) for d in range(DEPTH)])
    w1 = np.zeros((DEPTH, D, HT, 2, P), np.float32)
    w2 = np.zeros((DEPTH, HT * P, D), np.float32)
    for k in range(2):
        w = np.zeros((DEPTH, D, HT * P), np.float32)
        w[:, :, :HID] = i["L3_ffn_W1"][:, :, k * HID:(k + 1) * HID]
        w1[:, :, :, k] = w.reshape(DEPTH, D, HT, P)
    w2[:, :HID] = i["L3_ffn_W2"]
    a["w12"] = np.stack([np.concatenate([_layout(w1[d].reshape(D, -1)), _layout(w2[d])], 1) for d in range(DEPTH)])
    return a


def kernel(**inputs):
    import concourse.bacc as _bacc
    from concourse.bass_utils import run_bass_kernel_spmd as _run

    nc = _bacc.Bacc("TRN2", target_bir_lowering=False, num_devices=1)
    arrays = {f"in_{k}": v for k, v in lay_out(inputs).items()}
    aps = {k[3:]: nc.dram_tensor(k, v.shape, mybir.dt.from_np(v.dtype), kind="ExternalInput").ap() for k, v in arrays.items()}
    out = nc.dram_tensor("out_xT", (D, B, S), F32, kind="ExternalOutput").ap()
    build(nc, aps, out)
    r = _run(nc, [arrays], core_ids=[0])
    return np.ascontiguousarray(r.results[0]["out_xT"].transpose(1, 2, 0))
```

```python
from contextlib import ExitStack

import numpy as np

import concourse.bass as bass
from concourse import mybir

ALU = mybir.AluOpType
ACT = mybir.ActivationFunctionType
AX = mybir.AxisListType
F32 = mybir.dt.float32
F32R = mybir.dt.float32r
BF16 = mybir.dt.bfloat16
FP8 = mybir.dt.float8e4
U8 = mybir.dt.uint8
I32 = mybir.dt.int32

P = 128
B, S, S2, D = 4, 512, 1024, 256
C = D // P
H = 16
HD = D // H
QT = S // P
KT = S2 // P
G4 = H // 4
FF0 = 1024 // P
PAD = 8
ROW = PAD + S
EPS = 1e-5
RSQRT = 0.703952253
MASKED = -1e30
PIECE = S // 4
PAIRS = [(0, 0), (0, 1), (0, 2), (1, 0), (1, 1), (2, 0)]
STACK = len(PAIRS) * HD
DEPTH, LHD, WIN = 6, 64, 64
INNER = H * LHD
HID = int(D * 4 * 2 / 3)
HT = -(-HID // P)

VECS = {}
_n = 0
for _name, _w in (
    [("L0_bq", 2), ("L0_bk", 2), ("L0_bo", 2), ("L0_b1", FF0), ("L0_b2", 2),
     ("L1_bq", 2), ("L1_bk", 2), ("L1_bo", 2), ("L2_b", 2), ("mu_r", 2), ("mu_k", 2),
     ("L3_bq", 2), ("L3_bk", 2), ("L3_bo", 2), ("g_x", 4), ("g_f", 4), ("s_in", 1), ("s_k", 1)]
    + [(f"{n}{i}", w) for i in range(DEPTH)
       for n, w in (("ln_g", 2), ("ln_b", 2), ("b1a", HT), ("b1g", HT), ("b2", 2))]
):
    VECS[_name] = _n
    _n += _w
N_VECS = _n


def bc(ap, axis, n):
    dims = [list(d) for d in ap.ap]
    return bass.AP(ap.tensor, ap.offset, dims[:axis] + [[0, n]] + dims[axis:])


W1_JOBS, W2_JOBS = 5, 9


class Queue:

    def __init__(self, eng, sem):
        self.eng, self.sem, self.n, self.seen = eng, sem, 0, {}

    def wait(self, *marks):
        for m in marks:
            if isinstance(m, list):
                self.wait(*m)
            elif m is not None:
                sem, value = m
                if self.seen.get(id(sem), 0) < value:
                    self.eng.wait_ge(sem, value)
                    self.seen[id(sem)] = value

    def done(self, ins):
        self.n += 1
        ins.then_inc(self.sem, 1)
        return (self.sem, self.n)


class Slot:

    def __init__(self, ap, sem=None):
        self.ap, self.free, self.sem, self.n = ap, [], sem, 0

    def dma(self, ins):
        self.n += 16
        ins.then_inc(self.sem, 16)
        return (self.sem, self.n)


class Ring:

    def __init__(self, slots):
        self.slots = list(slots)
        self.low = len(self.slots)

    def take(self):
        return self.slots.pop(0)

    def give(self, slot, *marks):
        slot.free = list(marks)
        self.slots.append(slot)


class Banks:

    def __init__(self, ps):
        self.ps, self.order, self.free = ps, list(range(8)), [[] for _ in range(8)]

    def left(self, n):
        if n == 1:
            return len(self.order) > 0
        return any(b % 2 == 0 and b + 1 in self.order for b in self.order)

    def take(self, n=1):
        if n == 2:
            pairs = [b for b in range(0, 8, 2) if b in self.order and b + 1 in self.order]
            b = min(pairs, key=lambda b: max(self.order.index(b), self.order.index(b + 1)))
        else:
            single = [b for b in self.order if b ^ 1 not in self.order]
            b = (single or self.order)[0]
        for x in range(b, b + n):
            self.order.remove(x)
        s = Slot(self.ps[:, b, :] if n == 1 else self.ps[:, b:b + 2, :])
        s.bank, s.width = b, n
        s.free = [m for x in range(b, b + n) for m in self.free[x]]
        return s

    def give(self, slot, *marks):
        for x in range(slot.bank, slot.bank + slot.width):
            self.free[x] = list(marks)
            self.order.append(x)


def need(*wanted):
    while True:
        ok = True
        for w in wanted:
            if isinstance(w[0], Banks):
                banks, ones, pairs = w
                whole = sum(b in banks.order and b + 1 in banks.order for b in range(0, 8, 2))
                lone = len(banks.order) - 2 * whole
                ok &= whole >= pairs and lone + 2 * (whole - pairs) >= ones
            else:
                ok &= len(w[0].slots) >= w[1]
        if ok:
            return
        yield


def run_jobs(jobs, window):
    jobs = list(jobs)
    live, of_list = [], set()
    stuck = 0
    while jobs or live:
        while jobs and sum(j in of_list for j in live) < window:
            of_list.add(jobs[0])
            live.append(jobs.pop(0))
        for j in list(live):
            before = Progress.count
            try:
                next(j)
            except StopIteration:
                live.remove(j)
                Progress.count += 1
            stuck = 0 if Progress.count != before else stuck + 1
            live += Spawned.jobs
            Spawned.jobs = []
            if stuck > 50:
                raise RuntimeError("no job can go on: too few buffers")


class Spawned:
    jobs = []


def spawn(job):
    Spawned.jobs.append(job)


class Progress:
    count = 0


def build(nc, a, out, stages=99, depths=DEPTH):
    ctx = ExitStack()
    with ctx:
        def sem(name):
            return ctx.enter_context(nc.semaphore(name))

        def sb(name, shape, dt=F32, where=ctx):
            return where.enter_context(nc.sbuf_tensor(name, shape, dt))

        PE = Queue(nc.tensor, sem("pe_done"))
        V = Queue(nc.vector, sem("vector_done"))
        A = Queue(nc.scalar, sem("scalar_done"))
        G = Queue(nc.gpsimd, sem("gpsimd_done"))
        SP = Queue(nc.sync, sem("sync_done"))

        def count(q, ins):
            Progress.count += 1
            return q.done(ins)

        def v_(ins): return count(V, ins)
        def a_(ins): return count(A, ins)
        def g_(ins): return count(G, ins)
        def pe_(ins): return count(PE, ins)

        tensor, vector, scalar, gpsimd, sync = nc.tensor, nc.vector, nc.scalar, nc.gpsimd, nc.sync
        psum_all = ctx.enter_context(nc.psum_tensor("psum", [P, 8, 512], F32))
        banks = Banks(psum_all)

        X = sb("x_resid", [P, C, B, ROW])
        vecs = sb("vecs", [P, N_VECS])
        gates = sb("gates", [P, 8])
        ones_mean = sb("ones_mean", [P, P])
        ident = sb("ident", [P, P])
        ident_b = sb("ident_b", [P, P], BF16)
        small = sb("small", [P, 64])

        s_vec, s_x = sem("vecs_loaded"), sem("x_loaded")
        sync.dma_start(vecs[:, :], a["vecs"]).then_inc(s_vec, 16)
        sync.dma_start(ident[:, :], a["ident"]).then_inc(s_vec, 16)
        for c in range(C):
            sync.dma_start(X[:, c, :, PAD:ROW], a["xT"][c * P:(c + 1) * P, :, :]).then_inc(s_x, 16)
        vec_in, x_in = (s_vec, 32), (s_x, 16 * C)
        t_pad = v_(vector.memset(X[:, :, :, 0:PAD], 0.0))
        t_ones = v_(vector.memset(ones_mean[:, :], 1.0 / D))
        V.wait(vec_in)
        t_idb = v_(vector.tensor_copy(ident_b[:, :], ident[:, :]))
        A.wait(vec_in)
        t_gate = a_(scalar.activation(gates[:, 0:8], vecs[:, VECS["g_x"]:VECS["g_x"] + 8], ACT.Tanh))
        x_ready = [[x_in, t_pad] for _ in range(B)]

        def vec(name, i=0):
            return vecs[:, VECS[name] + i:VECS[name] + i + 1]

        V.wait(t_gate)
        small_at = {}

        def derived(name, width, fn):
            at = sum(w for _, w in small_at.values())
            small_at[name] = (at, width)
            return v_(fn(small[:, at:at + width]))

        def sm(name, i=0):
            at = small_at[name][0] + i
            return small[:, at:at + 1]

        V.wait(vec_in)
        v2 = lambda name, w=2: vecs[:, VECS[name]:VECS[name] + w]
        for L, gi in (("L0", 0), ("L1", 1), ("L3", 3)):
            derived(L + "_bq4", 2, lambda o, L=L: vector.tensor_scalar(o, v2(L + "_bq"), 0.25, None, ALU.mult))
            derived(L + "_gbo", 2, lambda o, L=L, gi=gi: vector.tensor_scalar(
                o, v2(L + "_bo"), gates[:, gi:gi + 1], None, ALU.mult))
        derived("L0_gb2", 2, lambda o: vector.tensor_scalar(o, v2("L0_b2"), gates[:, 4:5], None, ALU.mult))
        derived("om_r", 2, lambda o: vector.tensor_scalar(o, v2("mu_r"), -1.0, 1.0, ALU.mult, ALU.add))
        derived("om_k", 2, lambda o: vector.tensor_scalar(o, v2("mu_k"), -1.0, 1.0, ALU.mult, ALU.add))
        derived("inv_in", 1, lambda o: vector.reciprocal(o, vec("s_in")))
        derived("inv_k", 1, lambda o: vector.reciprocal(o, vec("s_k")))
        for d in range(DEPTH):
            derived(f"ln_gr{d}", 2, lambda o, d=d: vector.tensor_scalar(o, v2(f"ln_g{d}"), -RSQRT, None, ALU.mult))
        t_small = derived("s_both", 1, lambda o: vector.tensor_tensor(o, vec("s_in"), vec("s_k"), ALU.mult))
        for q in (V, A):
            q.wait(t_small, t_idb)
        PE.wait(t_ones, t_idb)

        x_kept = nc.dram_tensor("x_kept", [D, B, S], F32).ap()
        kept = [None] * B

        def tokens(b, c, shift=0):
            return X[:, c, b, PAD - shift:ROW - shift]

        def rsqrt(v, y, t):
            m = v_(vector.tensor_scalar(y.bitcast(I32), v.bitcast(I32), -0.5, float(0x5F1FFFF9), ALU.mult, ALU.add))
            V.wait(m)
            m = v_(vector.tensor_tensor(t, y, y, ALU.mult))
            V.wait(m)
            m = v_(vector.tensor_tensor(t, t, v, ALU.mult))
            V.wait(m)
            m = v_(vector.scalar_tensor_tensor(out=y, in0=t, scalar=-2.38924456, in1=y, op0=ALU.add, op1=ALU.mult))
            V.wait(m)
            m = v_(vector.tensor_tensor(t, y, y, ALU.mult))
            V.wait(m)
            m = v_(vector.scalar_tensor_tensor(out=t, in0=t, scalar=-0.5 * RSQRT * RSQRT, in1=v, op0=ALU.mult, op1=ALU.mult))
            V.wait(m)
            return v_(vector.scalar_tensor_tensor(out=y, in0=t, scalar=1.5 + 4e-7, in1=y, op0=ALU.add, op1=ALU.mult))

        def centred_rstd(b, shift, xc, work):
            yield from need((banks, 1, 0))
            mean = banks.take()
            PE.wait(x_ready[b], mean.free)
            for c in range(C):
                ins = tensor.matmul(mean.ap, ones_mean[:, :], tokens(b, c, shift * c), start=c == 0, stop=c == C - 1)
            t_mean = pe_(ins)
            yield
            V.wait(t_mean, xc.free, x_ready[b])
            for c in range(C):
                t_xc = v_(vector.tensor_tensor(xc.ap[:, c, PAD:ROW], tokens(b, c, shift * c), mean.ap, ALU.subtract))
            banks.give(mean, t_xc)
            yield from need((banks, 1, 0), (work, 3))
            sq0, sq1, tmp = work.take(), work.take(), work.take()
            A.wait(t_xc, sq0.free, sq1.free)
            for c, s in enumerate((sq0, sq1)):
                t_sq = a_(scalar.activation(s.ap, xc.ap[:, c, PAD:ROW], ACT.Square))
            yield
            yield from need((banks, 1, 0))
            var = banks.take()
            PE.wait(t_sq, var.free)
            for c, s in enumerate((sq0, sq1)):
                ins = tensor.matmul(var.ap, ones_mean[:, :], s.ap, start=c == 0, stop=c == C - 1)
            t_var = pe_(ins)
            yield
            V.wait(t_var, tmp.free)
            t = v_(vector.tensor_scalar(sq0.ap, var.ap, EPS, None, ALU.add))
            banks.give(var, t)
            V.wait(t)
            t_rs = rsqrt(sq0.ap, sq1.ap, tmp.ap)
            work.give(sq0, t_rs)
            work.give(tmp, t_rs)
            return sq1, t_rs

        def layer_norm(b, xn, work):
            rstd, t_rs = yield from centred_rstd(b, 0, xn, work)
            V.wait(t_rs)
            for c in range(C):
                t = v_(vector.scalar_tensor_tensor(out=xn.ap[:, c, PAD:ROW], in0=xn.ap[:, c, PAD:ROW], scalar=-RSQRT, in1=rstd.ap,
                                                   op0=ALU.mult, op1=ALU.mult))
            work.give(rstd, t)
            yield
            return t

        def first_part(p1):
            def psb(name, shape, dt=F32):
                return sb(name, shape, dt, p1)

            w_att = Slot(psb("w_att", [P, 10 * D])[:, :], sem("w_att_in"))
            w_ff = Slot(psb("w_ff", [P, 2 * FF0 * D])[:, :], sem("w_ff_in"))
            w_ffb = psb("w_ffb", [P, C, D], BF16)
            bias_b = psb("bias_b", [P, C], BF16)
            bv = psb("bv", [P, 3, D])
            ctxs = Ring(Slot(psb(f"ctx{i}", [P, C, S2])[:, :, :], sem(f"ctx_in{i}")) for i in range(1))
            norms = Ring(Slot(psb(f"xn{i}", [P, C, ROW])[:, :, :]) for i in range(2))
            works = Ring(Slot(psb(f"work{i}", [P, S])[:, :]) for i in range(6))
            parts = Ring(Slot(psb(f"parts{i}", [P, 3, S], BF16)[:, :, :], sem(f"parts_out{i}")) for i in range(2))
            stacks = Ring(Slot(psb(f"stack{i}", [P, 3 * S2])[:, :], sem(f"stack_in{i}")) for i in range(4))
            values = Ring([Slot(psb("values", [P, KT, H, 32])[:, :, :, :])])
            probs = Ring(Slot(psb(f"probs{i}", [P, 2, S])[:, :, :]) for i in range(6))
            outs = Ring(Slot(psb(f"attn{i}", [P, G4, S])[:, :, :]) for i in range(2))
            maxes = Ring(Slot(psb(f"max{i}", [P, 48])[:, :], sem(f"max_out{i}")) for i in range(4))
            shifts = Ring(Slot(psb(f"shift{i}", [16, 2, P], BF16)[:, :, :], sem(f"shift_out{i}")) for i in range(4))
            masks_q = Ring([Slot(psb("mask_by_query", [P, QT * S2], BF16)[:, :])])
            masks_k = Ring([Slot(psb("mask_by_key", [P, KT * S], BF16)[:, :])])
            mask_u8 = Ring(Slot(psb(f"mask_u8{i}", [P, S2], U8)[:, :], sem(f"mask_in{i}")) for i in range(2))
            q_dram = [Slot(nc.dram_tensor(f"q_parts{b}", [D, 3, S], BF16).ap()) for b in range(B)]
            k_dram = [Slot(nc.dram_tensor(f"k_parts{b}", [D, 3, S2], BF16).ap()) for b in range(B)]

            s_bv = sem("bv_in")
            sync.dma_start(bv[:, :, :], a["bv"]).then_inc(s_bv, 16)
            sync.dma_start(bias_b[:, :], a["L1f_bias"]).then_inc(s_bv, 16)
            bv_in = (s_bv, 32)
            V.wait(bv_in)
            for n in norms.slots:
                t_z = v_(vector.memset(n.ap[:, :, 0:PAD], 0.0))
            t_v1 = v_(vector.memset(values.slots[0].ap, 1.0))
            V.wait(t_z, t_v1)

            def load_weights(slot, name, width, after):
                SP.wait(after)
                Progress.count += 1
                return slot.dma(sync.dma_start(slot.ap[:, 0:width], a[name]))

            def cut(src, part, t_src):
                A.wait(t_src, part.free)
                t = a_(scalar.activation(part.ap[:, 0, :], src.ap, ACT.Copy))
                G.wait(t)
                t = g_(gpsimd.tensor_tensor(src.ap, src.ap, part.ap[:, 0, :], ALU.subtract))
                yield
                yield
                A.wait(t)
                t = a_(scalar.activation(part.ap[:, 1, :], src.ap, ACT.Copy))
                G.wait(t)
                return g_(gpsimd.tensor_tensor(part.ap[:, 2, :], src.ap, part.ap[:, 1, :], ALU.subtract))

            def load_mask(b, dst, by_query):
                V.wait(dst.free)
                for i in range(4):
                    yield from need((mask_u8, 1))
                    mu = mask_u8.take()
                    SP.wait(mu.free)
                    if by_query:
                        src, to_ = a["mask"][b, i * P:(i + 1) * P, :], mu.ap
                    else:
                        src = a["maskT"][b, 2 * i * P:(2 * i + 2) * P, :].rearrange("(t p) q -> p t q", p=P)
                        to_ = mu.ap.rearrange("p (t q) -> p t q", t=2)
                    t = mu.dma(sync.dma_start(to_, src))
                    V.wait(t)
                    t = v_(vector.tensor_scalar(dst.ap[:, i * S2:(i + 1) * S2], mu.ap, -1.0, -MASKED, ALU.add, ALU.mult))
                    mask_u8.give(mu, t)
                yield
                return t

            class Handed:

                made = loaded = 0

                def __init__(self):
                    self.ctx, self.groups, self.taken = None, [], []
                    self.number = Handed.made
                    Handed.made += 1

            def attention_maxima(b, L, w_in, to, mask=False):
                gi = int(L[1])
                wq = w_att.ap[:, 0:2 * D].rearrange("p (c n) -> p c n", c=C)
                wk = w_att.ap[:, 2 * D:4 * D].rearrange("p (c n) -> p c n", c=C)
                yield from need((ctxs, 1), (norms, 1))
                cx, xn = ctxs.take(), norms.take()
                SP.wait(cx.free)
                for c in range(C):
                    cx_in = cx.dma(sync.dma_start(cx.ap[:, c, :], a["ctxT"][c * P:(c + 1) * P, b, :]))
                t_xn = yield from layer_norm(b, xn, works)
                PE.wait(w_in, cx_in, t_xn)

                def project(w, src, m, n0, bias, scale, dram, after_reads):
                    yield from need((banks, 1, 0), (works, 1), (parts, 1))
                    ps, f, part = banks.take(), works.take(), parts.take()
                    PE.wait(ps.free)
                    for c in range(C):
                        ins = tensor.matmul(ps.ap, w[:, c, m * P:(m + 1) * P], src[c], start=c == 0, stop=c == C - 1)
                    t = pe_(ins)
                    A.wait(t, f.free)
                    t = a_(scalar.activation(f.ap, ps.ap, ACT.Identity, bias=bias, scale=scale))
                    banks.give(ps, t)
                    yield
                    t = yield from cut(f, part, t)
                    works.give(f, t)
                    SP.wait(t, after_reads)
                    mark = part.dma(sync.dma_start(dram.ap[m * P:(m + 1) * P, :, n0:n0 + S], part.ap))
                    parts.give(part, mark)
                    yield
                    return [mark]

                sent = []
                qd, kd = q_dram[b], k_dram[b]
                q_free, k_free = list(qd.free), list(kd.free)
                for m in range(C):
                    sent += yield from project(wq, [xn.ap[:, c, PAD:ROW] for c in range(C)], m, 0, sm(L + "_bq4", m), 0.25, qd, q_free)
                    for n in range(S2 // S):
                        sent += yield from project(wk, [cx.ap[:, c, n * S:(n + 1) * S] for c in range(C)], m, n * S,
                                                   vec(L + "_bk", m), 1.0, kd, k_free)
                norms.give(xn, (PE.sem, PE.n))
                to.ctx = cx
                if mask:
                    yield from need((masks_q, 1))
                    mq = masks_q.take()
                    t_mask = yield from load_mask(b, mq, True)
                    PE.wait(t_mask)
                group_reads = []

                def load_stack(g):
                    yield from need((stacks, 1))
                    st = stacks.take()
                    kst = st.ap[:, 0:2 * S2].bitcast(BF16).rearrange("p (h n) -> p h n", h=4)
                    qst = st.ap[:, 2 * S2:3 * S2].bitcast(BF16).rearrange("p (h n) -> p h n", h=4)
                    SP.wait(st.free, sent)
                    rows = slice(g * 4 * HD, (g + 1) * 4 * HD)
                    for i, (pq, pk) in enumerate(PAIRS):
                        sync.dma_start(qst[i * HD:(i + 1) * HD, :, :], qd.ap[rows, pq, :].rearrange("(h d) n -> d h n", d=HD)).then_inc(st.sem, 16)
                        sync.dma_start(kst[i * HD:(i + 1) * HD, :, :], kd.ap[rows, pk, :].rearrange("(h d) n -> d h n", d=HD)).then_inc(st.sem, 16)
                    sync.dma_start(kst[STACK:STACK + 2, :, :], a["ones"].rearrange("r (h n) -> r h n", h=4)).then_inc(st.sem, 16)
                    st.n += 16 * (2 * len(PAIRS) + 1)
                    group_reads.append((st.sem, st.n))
                    return st, kst, qst, (st.sem, st.n)

                def shift_rows(qst, mx, sh, t_mx, group):
                    if mask:
                        V.wait(t_mx)
                        t = v_(vector.tensor_scalar(mx.ap[:, 16:32], mx.ap[:, 0:16], 0.5 * MASKED, None, ALU.is_gt))
                        V.wait(t)
                        t = v_(vector.reciprocal(mx.ap[:, 16:32], mx.ap[:, 16:32]))
                        V.wait(t)
                        t = v_(vector.tensor_tensor(mx.ap[:, 32:48], mx.ap[:, 16:32], mx.ap[:, 16:32], ALU.subtract))
                        V.wait(t)
                        t_mx = v_(vector.tensor_tensor(mx.ap[:, 0:16], mx.ap[:, 0:16], mx.ap[:, 32:48], ALU.add))
                    yield
                    yield from need((banks, 1, 0))
                    ps = banks.take()
                    PE.wait(t_mx, ps.free)
                    t = pe_(tensor.transpose(ps.ap[0:16, 0:P], mx.ap[:, 0:16], ident[:, :]))
                    V.wait(t, sh.free)
                    t = v_(vector.tensor_scalar(sh.ap[:, 0, :], ps.ap[0:16, 0:P], -1.0, None, ALU.mult))
                    V.wait(t)
                    t = v_(vector.scalar_tensor_tensor(out=sh.ap[:, 1, :], in0=ps.ap[0:16, 0:P], scalar=-1.0, in1=sh.ap[:, 0, :],
                                                       op0=ALU.mult, op1=ALU.subtract))
                    maxes.give(mx, t)
                    banks.give(ps, t)
                    SP.wait(t)
                    for i in range(2):
                        dst = qst[STACK + i:STACK + i + 1, :, :].rearrange("r h (t q) -> r (h t) q", q=P)
                        sync.dma_start(dst, sh.ap[:, i, :]).then_inc(sh.sem, 16)
                    sh.n += 32
                    shifts.give(sh, (sh.sem, sh.n))
                    yield
                    yield
                    to.groups.append(group + ((sh.sem, sh.n),))

                while Handed.loaded < to.number:
                    yield
                coming = yield from load_stack(0)
                yield
                for g in range(G4):
                    st, kst, qst, st_in = coming
                    while len(to.taken) < g - 1:
                        yield
                    if g + 1 < G4:
                        coming = yield from load_stack(g + 1)
                    else:
                        Handed.loaded += 1
                    yield from need((maxes, 1), (shifts, 1))
                    mx, sh = maxes.take(), shifts.take()
                    V.wait(mx.free)
                    PE.wait(st_in)
                    for h in range(4):
                        for qt in range(QT):
                            yield from need((banks, 0, 1))
                            ps = banks.take(2)
                            PE.wait(ps.free)
                            for n in range(2):
                                ins = tensor.matmul(ps.ap[:, n, :], qst[0:STACK, h, qt * P:(qt + 1) * P], kst[0:STACK, h, n * S:(n + 1) * S],
                                                    start=True, stop=not mask)
                                if mask:
                                    ins = tensor.matmul(ps.ap[:, n, :], ident_b[:, :], mq.ap[:, qt * S2 + n * S:qt * S2 + (n + 1) * S],
                                                        start=False, stop=True)
                            t = pe_(ins)
                            V.wait(t)
                            at_ = h * QT + qt
                            t_mx = v_(vector.tensor_reduce(mx.ap[:, at_:at_ + 1], ps.ap, AX.XY, ALU.max))
                            banks.give(ps, t_mx)
                            yield
                    spawn(shift_rows(qst, mx, sh, t_mx, (st, kst, qst)))
                qd.free = kd.free = group_reads
                if mask:
                    masks_q.give(mq, (PE.sem, PE.n))

            def attention_values(b, L, w_in, given, done, mask=False):
                gi = int(L[1])
                wv = w_att.ap[:, 4 * D:6 * D].rearrange("p (c n) -> p c n", c=C)
                wo = w_att.ap[:, 6 * D:10 * D].rearrange("p (g n) -> p g n", g=G4)
                while given.ctx is None:
                    yield
                cx = given.ctx
                yield from need((values, 1))
                va = values.take()
                for kt in range(0, KT, 2):
                    yield from need((banks, 1, 0))
                    ps = banks.take()
                    PE.wait(ps.free)
                    for k in range(2):
                        for c in range(C):
                            ins = tensor.matmul(ps.ap[:, k * D:(k + 1) * D], cx.ap[:, c, (kt + k) * P:(kt + k + 1) * P],
                                                wv[:, c, :], start=c == 0, stop=c == C - 1)
                    t = pe_(ins)
                    V.wait(t, va.free)
                    for k in range(2):
                        t_va = v_(vector.tensor_tensor(
                            va.ap[:, kt + k, :, 0:HD], ps.ap[:, k * D:(k + 1) * D].rearrange("p (h d) -> p h d", h=H),
                            bv[:, (0, 1, None, 2)[gi], :].rearrange("p (h d) -> p h d", h=H), ALU.add))
                    banks.give(ps, t_va)
                    yield
                ctxs.give(cx, (PE.sem, PE.n))

                if mask:
                    yield from need((masks_k, 1))
                    mk = masks_k.take()
                    t_mask = yield from load_mask(b, mk, False)
                    PE.wait(t_mask)
                yield from need((outs, 1))
                at, t_at = outs.take(), []
                for g in range(G4):
                    while len(given.groups) <= g:
                        yield
                    st, kst, qst, sh_in = given.groups[g]
                    given.taken.append(g)
                    accs, waiting = [], []

                    def product(kt2, held, accs, g):
                        if not accs:
                            yield from need((banks, 1, 0))
                            accs.append(banks.take())
                        acc = accs[0]
                        PE.wait([m for _, m in held], acc.free)
                        for k in range(2):
                            for h in range(4):
                                kt = 2 * kt2 + k
                                ins = tensor.matmul(acc.ap[32 * h:32 * h + 32, :], va.ap[:, kt, 4 * g + h, :], held[h][0].ap[:, k, :],
                                                    start=kt == 0, stop=kt == KT - 1)
                        t = pe_(ins)
                        for p, _ in held:
                            probs.give(p, t)
                        return t

                    PE.wait(sh_in, t_va)
                    for kt2 in range(KT // 2):
                        held = []
                        for h in range(4):
                            yield from need((banks, 0, 1), (probs, 1))
                            ps, pr = banks.take(2), probs.take()
                            PE.wait(ps.free)
                            for k in range(2):
                                kt = 2 * kt2 + k
                                ins = tensor.matmul(ps.ap[:, k, :], kst[0:STACK + 2, h, kt * P:(kt + 1) * P], qst[0:STACK + 2, h, :],
                                                    start=True, stop=not mask)
                                if mask:
                                    ins = tensor.matmul(ps.ap[:, k, :], ident_b[:, :], mk.ap[:, kt * S:(kt + 1) * S],
                                                        start=False, stop=True)
                            t = pe_(ins)
                            A.wait(t, pr.free)
                            t = a_(scalar.activation(pr.ap, ps.ap, ACT.Exp))
                            banks.give(ps, t)
                            held.append((pr, t))
                            if h == 1 and waiting:
                                yield from product(*waiting.pop(0), accs, g)
                            yield
                        waiting.append((kt2, held))
                    stacks.give(st, (PE.sem, PE.n))

                    def tail(g, last, accs, product):
                        yield
                        yield
                        t = yield from product(*last, accs, g)
                        yield
                        yield from need((works, 1))
                        w, acc = works.take(), accs[0]
                        A.wait(t, at.free)
                        t = a_(scalar.activation(at.ap[:, g, :], acc.ap, ACT.Copy))
                        banks.give(acc, t)
                        yield
                        V.wait(t, w.free)
                        t = v_(vector.stream_shuffle(w.ap, at.ap[:, g, :], [16 + i % 16 for i in range(32)]))
                        V.wait(t)
                        for n0 in range(0, S, PIECE):
                            yield
                            t = v_(vector.reciprocal(w.ap[:, n0:n0 + PIECE], w.ap[:, n0:n0 + PIECE]))
                        G.wait(t)
                        t_at.append(g_(gpsimd.tensor_tensor(at.ap[:, g, :], at.ap[:, g, :], w.ap, ALU.mult)))
                        works.give(w, t_at[-1])
                        yield

                    spawn(tail(g, waiting.pop(0), accs, product))
                while len(t_at) < G4:
                    yield
                yield
                values.give(va, (PE.sem, PE.n))
                if mask:
                    masks_k.give(mk, (PE.sem, PE.n))
                yield
                PE.wait(t_at)
                for m in range(C):
                    yield from need((banks, 1, 0))
                    ps = banks.take()
                    PE.wait(ps.free)
                    for g in range(G4):
                        ins = tensor.matmul(ps.ap, wo[:, g, m * P:(m + 1) * P], at.ap[:, g, :], start=g == 0, stop=g == G4 - 1)
                    t = pe_(ins)
                    t = yield from gated_add(b, m, ps, t, gates[:, gi:gi + 1], sm(L + "_gbo", m))
                x_ready[b] = [t]
                outs.give(at, (PE.sem, PE.n))
                done.append((PE.sem, PE.n))

            def gated_add(b, m, ps, t, gate, gated_bias):
                yield from need((works, 1))
                w = works.take()
                A.wait(t, w.free)
                t = a_(scalar.activation(w.ap, ps.ap, ACT.Identity, bias=gated_bias, scale=gate))
                banks.give(ps, t)
                yield
                V.wait(t)
                t = v_(vector.tensor_tensor(tokens(b, m), tokens(b, m), w.ap, ALU.add))
                works.give(w, t)
                yield
                return t

            def binarize(w_in, done):
                halves = [(w_ff.ap[:, 0:FF0 * D].rearrange("p (c n) -> p c n", c=C), C, FF0 * P, 1.0),
                          (w_ff.ap[:, FF0 * D:2 * FF0 * D].rearrange("p (c n) -> p c n", c=FF0), FF0, D, D / (FF0 * P))]
                A.wait(w_in)
                V.wait(w_in)
                for w, nc_, width, extra in halves:
                    for n0 in range(0, width, 512):
                        n = min(512, width - n0)
                        yield from need((banks, 1, 0), (works, 2))
                        ps, ab, sg = banks.take(), works.take(), works.take()
                        PE.wait(ps.free)
                        t = None
                        for c in range(nc_):
                            A.wait(ab.free, t)
                            t = a_(scalar.activation(ab.ap[:, 0:n], w[:, c, n0:n0 + n], ACT.Abs))
                            PE.wait(t)
                            t = pe_(tensor.matmul(ps.ap[:, 0:n], ones_mean[:, :], ab.ap[:, 0:n], start=c == 0, stop=c == nc_ - 1))
                        A.wait(t)
                        t = a_(scalar.activation(ab.ap[:, 0:n], ps.ap[:, 0:n], ACT.Copy, scale=extra))
                        banks.give(ps, t)
                        V.wait(t)
                        for c in range(nc_):
                            A.wait(sg.free)
                            t = a_(scalar.activation(sg.ap[:, 0:n], w[:, c, n0:n0 + n], ACT.Sign))
                            V.wait(t)
                            t = v_(vector.tensor_tensor(sg.ap[:, 0:n], sg.ap[:, 0:n], ab.ap[:, 0:n], ALU.mult))
                            V.wait(t)
                            t = v_(vector.tensor_tensor(sg.ap[:, 0:n], sg.ap[:, 0:n], w[:, c, n0:n0 + n], ALU.subtract))
                            V.wait(t)
                            t = v_(vector.tensor_tensor(w[:, c, n0:n0 + n], w[:, c, n0:n0 + n], sg.ap[:, 0:n], ALU.add))
                            sg.free = [t]
                        works.give(ab, t)
                        works.give(sg, t)
                        yield
                done.append(t)

            def feed_forward0(b, w_ready, done):
                w1 = w_ff.ap[:, 0:FF0 * D].rearrange("p (c n) -> p c n", c=C)
                w2 = w_ff.ap[:, FF0 * D:2 * FF0 * D].rearrange("p (k n) -> p k n", k=FF0)
                yield from need((norms, 1))
                xn = norms.take()
                t_xn = yield from layer_norm(b, xn, works)
                while not w_ready:
                    yield
                yield from need((banks, 2, 0))
                acc = [banks.take() for _ in range(C)]
                PE.wait(w_ready, t_xn, acc[0].free, acc[1].free)
                before = None
                for i in range(FF0 + 1):
                    if i < FF0:
                        yield from need((banks, 1, 0), (works, 1))
                        ps, h = banks.take(), works.take()
                        PE.wait(ps.free)
                        for c in range(C):
                            ins = tensor.matmul(ps.ap, w1[:, c, i * P:(i + 1) * P], xn.ap[:, c, PAD:ROW], start=c == 0, stop=c == C - 1)
                        t = pe_(ins)
                        A.wait(t, h.free)
                        t_h = a_(scalar.activation(h.ap, ps.ap, ACT.Gelu, bias=vec("L0_b1", i)))
                        banks.give(ps, t_h)
                    if before is not None:
                        k, hb, t_hb = before
                        PE.wait(t_hb)
                        for m in range(C):
                            ins = tensor.matmul(acc[m].ap, w2[:, k, m * P:(m + 1) * P], hb.ap, start=k == 0, stop=k == FF0 - 1)
                        t = pe_(ins)
                        works.give(hb, t)
                    before = (i, h, t_h) if i < FF0 else None
                    yield
                norms.give(xn, (PE.sem, PE.n))
                t_acc = t
                for m in range(C):
                    t = yield from gated_add(b, m, acc[m], t_acc, gates[:, 4:5], sm("L0_gb2", m))
                x_ready[b] = [t]
                done.append((PE.sem, PE.n))

            def quantize(src, dst, inv, w):
                n = src.shape[-1]
                val, big, aux = (x.ap[:, 0:n] for x in w[:3])
                lo8, hi8 = w[3].ap.bitcast(FP8)[:, 0:n], w[3].ap.bitcast(FP8)[:, S:S + n]
                t = v_(vector.tensor_scalar(val, src, inv, None, ALU.mult))
                V.wait(t)
                v_(vector.tensor_scalar(lo8, val, 240.0, -240.0, ALU.min, ALU.max, saturate=False))
                t = v_(vector.tensor_scalar(aux, val, 0.5, 240.0, ALU.mult, ALU.min))
                V.wait(t)
                t = v_(vector.tensor_scalar(hi8, aux, -240.0, None, ALU.max, saturate=False))
                V.wait(t)
                t = v_(vector.scalar_tensor_tensor(out=big, in0=hi8, scalar=2.0, in1=lo8, op0=ALU.mult, op1=ALU.subtract))
                t = v_(vector.scalar_tensor_tensor(out=val, in0=val, scalar=-1.0, in1=val, op0=ALU.mult, op1=ALU.max))
                V.wait(t)
                t = v_(vector.scalar_tensor_tensor(out=big, in0=val, scalar=16.0, in1=big, op0=ALU.is_ge, op1=ALU.mult))
                t = v_(vector.tensor_scalar(val, val, 464.0, None, ALU.is_le))
                V.wait(t)
                t = v_(vector.reciprocal(aux, val))
                t2 = v_(vector.tensor_tensor(big, big, lo8, ALU.add))
                V.wait(t, t2)
                t = v_(vector.tensor_tensor(aux, aux, aux, ALU.subtract))
                V.wait(t)
                return v_(vector.tensor_tensor(dst, big, aux, ALU.add))

            def quantize_weights(done):
                yield from need((works, 4))
                w = [works.take() for _ in range(4)]
                s_k8 = sem("kernel_in")
                m = (s_k8, 16)
                SP.wait(*[x.free for x in w])
                sync.dma_start(w_ffb[:, :, :], a["L1f_w"]).then_inc(s_k8, 16)
                V.wait(m, *[x.free for x in w])
                flat = w_ffb[:, :, :].rearrange("p c n -> p (c n)")
                t = quantize(flat, flat, sm("inv_k"), w)
                for x in w:
                    works.give(x, t)
                yield
                done.append(t)

            def feed_forward1(b, w_ready, done):
                yield from need((norms, 1))
                xn = norms.take()
                t_xn = yield from layer_norm(b, xn, works)
                while not w_ready:
                    yield
                yield from need((works, 4), (parts, 1))
                w, part = [works.take() for _ in range(4)], parts.take()
                V.wait(t_xn, part.free, *[x.free for x in w])
                for c in range(C):
                    t = v_(vector.tensor_copy(part.ap[:, 2, :], xn.ap[:, c, PAD:ROW]))
                    V.wait(t)
                    t = quantize(part.ap[:, 2, :], part.ap[:, c, :], sm("inv_in"), w)
                    V.wait(t)
                    yield
                norms.give(xn, t)
                for x in w:
                    works.give(x, t)
                PE.wait(t, w_ready)
                for m in range(C):
                    yield from need((banks, 1, 0), (works, 1))
                    ps, y = banks.take(), works.take()
                    PE.wait(ps.free)
                    for c in range(C):
                        ins = tensor.matmul(ps.ap, w_ffb[:, c, m * P:(m + 1) * P], part.ap[:, c, :], start=c == 0, stop=c == C - 1)
                    t = pe_(ins)
                    yb = y.ap.bitcast(BF16)
                    V.wait(t, y.free)
                    t = v_(vector.tensor_scalar(yb[:, 0:S], ps.ap, sm("s_both"), None, ALU.mult))
                    banks.give(ps, t)
                    V.wait(t)
                    t = v_(vector.tensor_scalar(yb[:, S:2 * S], yb[:, 0:S], bias_b[:, m:m + 1], None, ALU.add))
                    V.wait(t)
                    t = v_(vector.scalar_tensor_tensor(out=tokens(b, m), in0=yb[:, S:2 * S], scalar=gates[:, 5:6], in1=tokens(b, m),
                                                       op0=ALU.mult, op1=ALU.add))
                    works.give(y, t)
                    yield
                parts.give(part, (PE.sem, PE.n))
                x_ready[b] = [t]
                done.append((PE.sem, PE.n))

            def attention_single(b, w_in, done):
                wt = w_att.ap[:, 0:2 * D].rearrange("p (c n) -> p c n", c=C)
                yield from need((ctxs, 1), (norms, 1), (stacks, 2))
                cx, xn, st, raw = ctxs.take(), norms.take(), stacks.take(), stacks.take()
                SP.wait(cx.free, raw.free)
                for c in range(C):
                    cx_in = cx.dma(sync.dma_start(cx.ap[:, c, :], a["ctxT"][c * P:(c + 1) * P, b, :]))
                ctok = raw.ap[:, 0:2 * S2].rearrange("p (t n) -> p t n", t=KT)
                ctok_in = raw.dma(sync.dma_start(ctok, a["ctx"][b].rearrange("(t p) n -> p t n", p=P)))
                t_xn = yield from layer_norm(b, xn, works)
                eo = st.ap[:, 0:2 * S2].rearrange("p (c n) -> p c n", c=C)
                ex = st.ap[:, 2 * S2:3 * S2].rearrange("p (c n) -> p c n", c=C)
                PE.wait(w_in, cx_in, t_xn)
                A.wait(st.free)
                for m in range(C):
                    for n in range(3):
                        yield from need((banks, 1, 0))
                        ps = banks.take()
                        PE.wait(ps.free)
                        for c in range(C):
                            src = xn.ap[:, c, PAD:ROW] if n == 2 else cx.ap[:, c, n * S:(n + 1) * S]
                            ins = tensor.matmul(ps.ap, wt[:, c, m * P:(m + 1) * P], src, start=c == 0, stop=c == C - 1)
                        t = pe_(ins)
                        A.wait(t)
                        dst = ex[:, m, :] if n == 2 else eo[:, m, n * S:(n + 1) * S]
                        t_e = a_(scalar.activation(dst, ps.ap, ACT.Identity, bias=vec("L2_b", m)))
                        banks.give(ps, t_e)
                        yield
                ctxs.give(cx, (PE.sem, PE.n))
                norms.give(xn, (PE.sem, PE.n))
                PE.wait(t_e, ctok_in)
                for qt in range(QT):
                    yield from need((banks, 0, 1), (probs, 2), (maxes, 1))
                    ps, pr, pt, mx = banks.take(2), probs.take(), probs.take(), maxes.take()
                    PE.wait(ps.free)
                    for n in range(2):
                        for c in range(C):
                            ins = tensor.matmul(ps.ap[:, n, :], ex[:, c, qt * P:(qt + 1) * P], eo[:, c, n * S:(n + 1) * S],
                                                start=c == 0, stop=c == C - 1)
                    t = pe_(ins)
                    V.wait(t, mx.free)
                    t = v_(vector.tensor_reduce(mx.ap[:, 0:1], ps.ap, AX.XY, ALU.max, negate=True))
                    yield
                    A.wait(t, pr.free)
                    t = a_(scalar.activation(pr.ap, ps.ap, ACT.Exp, bias=mx.ap[:, 0:1], accum_out=mx.ap[:, 1:2]))
                    banks.give(ps, t)
                    V.wait(t)
                    t = v_(vector.reciprocal(mx.ap[:, 2:3], mx.ap[:, 1:2]))
                    V.wait(t)
                    t_p = v_(vector.tensor_scalar(pr.ap, pr.ap, mx.ap[:, 2:3], None, ALU.mult))
                    maxes.give(mx, t_p)
                    yield
                    yield from need((banks, 0, 1))
                    ps = banks.take(2)
                    PE.wait(t_p, ps.free)
                    for kt in range(KT):
                        ins = tensor.transpose(ps.ap[:, kt // 4, (kt % 4) * P:(kt % 4 + 1) * P],
                                               pr.ap[:, kt // 4, (kt % 4) * P:(kt % 4 + 1) * P], ident[:, :])
                    t = pe_(ins)
                    probs.give(pr, t)
                    A.wait(t, pt.free)
                    t = a_(scalar.activation(pt.ap, ps.ap, ACT.Copy))
                    banks.give(ps, t)
                    yield
                    yield from need((banks, 1, 0))
                    ps = banks.take()
                    PE.wait(t, ps.free)
                    for m in range(C):
                        for kt in range(KT):
                            ins = tensor.matmul(ps.ap[:, m * P:(m + 1) * P], ctok[:, kt, m * P:(m + 1) * P],
                                                pt.ap[:, kt // 4, (kt % 4) * P:(kt % 4 + 1) * P], start=kt == 0, stop=kt == KT - 1)
                    t = pe_(ins)
                    probs.give(pt, t)
                    V.wait(t, t_xn)
                    for m in range(C):
                        xs = X[:, m, b, PAD + qt * P:PAD + (qt + 1) * P]
                        t_x = v_(vector.scalar_tensor_tensor(out=xs, in0=ps.ap[:, m * P:(m + 1) * P], scalar=gates[:, 2:3], in1=xs,
                                                             op0=ALU.mult, op1=ALU.add))
                    banks.give(ps, t_x)
                    yield
                stacks.give(st, (PE.sem, PE.n))
                stacks.give(raw, (PE.sem, PE.n))
                x_ready[b] = [t_x]
                done.append((PE.sem, PE.n))

            def feed_forward2(b, w_in, done):
                w3 = w_ff.ap[:, 0:6 * D].rearrange("p (w c n) -> p w c n", w=3, c=C)
                yield from need((norms, 1))
                xn = norms.take()
                t_xn = yield from layer_norm(b, xn, works)
                yield from need((outs, 1), (norms, 1))
                mixed, kact = outs.take(), norms.take()
                V.wait(t_xn, mixed.free, kact.free)
                for i, (mu, om) in enumerate((("mu_r", "om_r"), ("mu_k", "om_k"))):
                    for c in range(C):
                        dst = mixed.ap[:, 2 * i + c, :]
                        t = v_(vector.tensor_scalar(dst, xn.ap[:, c, PAD - 1:ROW - 1], sm(om, c), None, ALU.mult))
                        V.wait(t)
                        t = v_(vector.scalar_tensor_tensor(out=dst, in0=xn.ap[:, c, PAD:ROW], scalar=vec(mu, c), in1=dst,
                                                           op0=ALU.mult, op1=ALU.add))
                norms.give(xn, t)
                yield
                PE.wait(t, w_in)
                for m in range(C):
                    yield from need((banks, 1, 0))
                    ps = banks.take()
                    PE.wait(ps.free)
                    for c in range(C):
                        ins = tensor.matmul(ps.ap, w3[:, 1, c, m * P:(m + 1) * P], mixed.ap[:, 2 + c, :], start=c == 0, stop=c == C - 1)
                    t = pe_(ins)
                    V.wait(t)
                    t = v_(vector.tensor_scalar(kact.ap[:, m, PAD:ROW], ps.ap, 0.0, None, ALU.max))
                    banks.give(ps, t)
                    A.wait(t)
                    t_k = a_(scalar.activation(kact.ap[:, m, PAD:ROW], kact.ap[:, m, PAD:ROW], ACT.Square))
                    yield
                for m in range(C):
                    yield from need((banks, 2, 0), (works, 1))
                    pr, pk, sg = banks.take(), banks.take(), works.take()
                    PE.wait(pr.free, pk.free)
                    for c in range(C):
                        ins = tensor.matmul(pr.ap, w3[:, 0, c, m * P:(m + 1) * P], mixed.ap[:, c, :], start=c == 0, stop=c == C - 1)
                    t = pe_(ins)
                    V.wait(t, sg.free)
                    t = v_(vector.tensor_scalar(sg.ap, pr.ap, -80.0, None, ALU.max))
                    banks.give(pr, t)
                    A.wait(t)
                    t = a_(scalar.activation(sg.ap, sg.ap, ACT.Exp, scale=-1.0))
                    V.wait(t)
                    t = v_(vector.tensor_scalar(sg.ap, sg.ap, 1.0, None, ALU.add))
                    V.wait(t)
                    t_s = v_(vector.reciprocal(sg.ap, sg.ap))
                    PE.wait(t_k)
                    for c in range(C):
                        ins = tensor.matmul(pk.ap, w3[:, 2, c, m * P:(m + 1) * P], kact.ap[:, c, PAD:ROW], start=c == 0, stop=c == C - 1)
                    t = pe_(ins)
                    V.wait(t, t_s)
                    t = v_(vector.tensor_tensor(sg.ap, pk.ap, sg.ap, ALU.mult))
                    banks.give(pk, t)
                    V.wait(t)
                    t = v_(vector.scalar_tensor_tensor(out=tokens(b, m), in0=sg.ap, scalar=gates[:, 6:7], in1=tokens(b, m),
                                                       op0=ALU.mult, op1=ALU.add))
                    works.give(sg, t)
                    yield
                outs.give(mixed, (PE.sem, PE.n))
                norms.give(kact, (PE.sem, PE.n))
                x_ready[b] = [t]
                done.append((PE.sem, PE.n))

            def put_aside(b, done):
                yield from need((norms, 1))
                xn = norms.take()
                SP.wait(x_ready[b])
                s_keep = sem(f"kept{b}")
                for c in range(C):
                    sync.dma_start(x_kept[c * P:(c + 1) * P, b, :], tokens(b, c)).then_inc(s_keep, 16)
                kept[b] = (s_keep, 16 * C)
                t_xn = yield from layer_norm(b, xn, works)
                V.wait(t_xn, kept[b], (PE.sem, PE.n))
                for c in range(C):
                    t = v_(vector.tensor_copy(tokens(b, c), xn.ap[:, c, PAD:ROW]))
                norms.give(xn, t)
                x_ready[b] = [t]
                done.append(t)
                yield

            def loader(slot, name, width, users, box):
                while len(users) < (B if users is not NONE else 0):
                    yield
                box.append(load_weights(slot, name, width, list(users)))

            NONE = []
            jobs, turn, layer_no = [], [0] * B, [0]

            def layer(name, job, slot, wname, width, before, prepare=None):
                box, ready, done = [], [], []
                if wname:
                    jobs.append(loader(slot, wname, width, before, box))
                if prepare:
                    jobs.append(prepare(box, ready))
                layer_no[0] += 1
                for b in range(B):
                    halves = job(b, box, ready, done)
                    for half in halves:
                        jobs.append(in_turn(b, layer_no[0], half, half is halves[-1]))
                return done

            def in_turn(b, number, job, last):
                while turn[b] != number - 1:
                    yield
                yield from job
                if last:
                    turn[b] = number

            def wait_box(box):
                while not box:
                    yield

            def with_box(fn):
                def job(b, box, ready, done):
                    def late():
                        yield from wait_box(box)
                        yield from fn(b, box[0], done)
                    return [late()]
                return job

            def attention(L, mask=False):
                def job(b, box, ready, done):
                    to = Handed()

                    def first():
                        yield from wait_box(box)
                        yield from attention_maxima(b, L, box[0], to, mask)

                    def second():
                        yield from wait_box(box)
                        yield from attention_values(b, L, box[0], to, done, mask)
                    return [first(), second()]
                return job

            def prep(fn):
                def job(box, ready):
                    def late():
                        yield from wait_box(box)
                        yield from fn(box[0], ready)
                    return late()
                return job

            A.wait(t_gate)
            V.wait(t_gate)
            users_att, users_ff = NONE, NONE
            if stages >= 1:
                users_att = layer("L0x", attention("L0"), w_att, "L0_att", 10 * D, users_att)
            if stages >= 2:
                users_ff = layer("L0f", lambda b, box, ready, d: [feed_forward0(b, ready, d)], w_ff, "L0_ff", 2 * FF0 * D, users_ff,
                                 prep(binarize))
            if stages >= 3:
                users_att = layer("L1x", attention("L1", mask=True), w_att, "L1_att", 10 * D, users_att)
            if stages >= 4:
                layer("L1f", lambda b, box, ready, d: [feed_forward1(b, ready, d)], None, None, 0, None,
                      lambda box, ready: quantize_weights(ready))
            if stages >= 5:
                users_att = layer("L2x", with_box(lambda b, m, d: attention_single(b, m, d)), w_att, "L2_att", 2 * D, users_att)
            if stages >= 6:
                users_ff = layer("L2f", with_box(lambda b, m, d: feed_forward2(b, m, d)), w_ff, "L2_ff", 6 * D, users_ff)
            if stages >= 7:
                users_att = layer("L3x", attention("L3"), w_att, "L3_att", 10 * D, users_att)
            if stages >= 8:
                layer("norm", lambda b, box, ready, d: [put_aside(b, d)], None, None, 0, None)
            run_jobs(jobs, W1_JOBS)
            SP.wait(*[(s.sem, s.n) for s in parts.slots])

        with ExitStack() as p1:
            first_part(p1)

        def last_part(p2):
            def psb(name, shape, dt=F32):
                return sb(name, shape, dt, p2)

            every = [(q.sem, q.n) for q in (PE, V, A, G)]
            for q in (PE, V, A, G, SP):
                q.wait(*every)

            QW = C * 3 * 4 * LHD + 2 * D
            FW = C * 2 * HT * P + HT * D
            xs_hi, xs_lo = psb("xs_hi", [P, C, B, S], F32R), psb("xs_lo", [P, C, B, S], F32R)
            quads = Ring(Slot((psb(f"quad_hi{i}", [P, QW], F32R), psb(f"quad_lo{i}", [P, QW], F32R))) for i in range(2))
            w12 = Slot((psb("w12_hi", [P, FW], F32R), psb("w12_lo", [P, FW], F32R)))
            staged = Ring(Slot(psb(f"staged{i}", [P, 1024])[:, :], sem(f"staged_in{i}")) for i in range(2))
            rot = Slot(psb("rotary", [P, 2, QT, 2, LHD])[:, :, :, :, :])
            band = psb("band_bias", [P, 2 * P], BF16)
            keys = Ring(Slot(psb(f"keys{i}", [P, C, ROW])[:, :, :]) for i in range(2))
            vals = Ring(Slot(psb(f"vals{i}", [P, QT, 4 * LHD])[:, :, :]) for i in range(2))
            queries = Ring(Slot(psb(f"queries{i}", [P, 4, P])[:, :, :]) for i in range(3))
            pairs = Ring(Slot((psb(f"pair_hi{i}", [P, C, S], F32R), psb(f"pair_lo{i}", [P, C, S], F32R))) for i in range(2))
            hids = Ring(Slot((psb(f"hid_hi{i}", [P, S], F32R), psb(f"hid_lo{i}", [P, S], F32R))) for i in range(2))
            probs = Ring(Slot(psb(f"lprobs{i}", [P, 4, 2 * P])[:, :, :]) for i in range(2))
            works = Ring(Slot(psb(f"lwork{i}", [P, S])[:, :]) for i in range(6))
            turned = Ring(Slot(psb(f"turned{i}", [P, S])[:, :]) for i in range(2))
            stats = Ring(Slot(psb(f"stat{i}", [P, 24])[:, :]) for i in range(8))

            s_c2 = sem("constants_in")
            sync.dma_start(band[:, :], a["band"]).then_inc(s_c2, 16)
            c2_in = (s_c2, 16)
            PE.wait(c2_in)
            V.wait(c2_in)
            for q_ in queries.slots:
                for h in range(4):
                    lo = 64 * (1 - h % 2)
                    t = v_(vector.memset(q_.ap[lo:lo + 64, h, :], 0.0))
            for p_ in probs.slots:
                t = v_(vector.memset(p_.ap[:, :, 0:64], 0.0))
            PE.wait(t)
            V.wait(t)
            G.wait(t)

            def split3(ps, wh, wl, xh, xl, start, stop, w_moves=False):
                order = [(wh, xh), (wh, xl), (wl, xh)] if not w_moves else [(xh, wh), (xh, wl), (xl, wh)]
                for n, (l, r) in enumerate(order):
                    ins = tensor.matmul(ps, l, r, start=start and n == 0, stop=stop and n == 2)
                return ins

            def load_split(dst, src, width, after, box):
                hi, lo = dst
                for n0 in range(0, width, 1024):
                    n = min(1024, width - n0)
                    yield from need((staged, 1))
                    s = staged.take()
                    SP.wait(s.free)
                    t = s.dma(sync.dma_start(s.ap[:, 0:n], src[:, n0:n0 + n]))
                    V.wait(t, after)
                    t = v_(vector.tensor_copy(hi[:, n0:n0 + n], s.ap[:, 0:n]))
                    G.wait(t)
                    t = g_(gpsimd.tensor_tensor(lo[:, n0:n0 + n], s.ap[:, 0:n], hi[:, n0:n0 + n].bitcast(F32), ALU.subtract))
                    staged.give(s, t)
                    yield
                box.append(t)

            xs_mark = [None] * B
            xs_read = [[] for _ in range(B)]

            def split_tokens(b):
                A.wait(x_ready[b], xs_read[b])
                for c in range(C):
                    t = a_(scalar.activation(xs_hi[:, c, b, :], tokens(b, c, c), ACT.Copy))
                G.wait(t, x_ready[b])
                for c in range(C):
                    t = g_(gpsimd.tensor_tensor(xs_lo[:, c, b, :], tokens(b, c, c), xs_hi[:, c, b, :].bitcast(F32), ALU.subtract))
                xs_mark[b] = t

            def rotary_tables(d, after, box):
                yield from need((staged, 2))
                tab, sc = staged.take(), staged.take()
                SP.wait(sc.free, tab.free)
                scales = sc.ap[:, 0:2 * LHD].rearrange("p (s d) -> p s d", s=2)
                t_s = sc.dma(sync.dma_start(scales, a["qk_scale"][d]))
                base = tab.ap.rearrange("p (f t s d) -> p f t s d", f=2, t=QT, s=2)
                t_b = tab.dma(sync.dma_start(base, a["rotary"]))
                V.wait(t_s, t_b, after)
                h = LHD // 2
                v_(vector.tensor_tensor(rot.ap[:, 0], base[:, 0], bc(scales, 1, QT), ALU.mult))
                v_(vector.tensor_tensor(rot.ap[:, 1, :, :, 0:h], base[:, 1, :, :, 0:h], bc(scales[:, :, h:LHD], 1, QT), ALU.mult))
                t = v_(vector.tensor_tensor(rot.ap[:, 1, :, :, h:LHD], base[:, 1, :, :, h:LHD], bc(scales[:, :, 0:h], 1, QT), ALU.mult))
                staged.give(tab, t)
                staged.give(sc, t)
                box.append(t)
                yield

            COLS = 3 * 4 * LHD

            def columns(w, c, lo, hi):
                return w[:, c * COLS + lo:c * COLS + hi]

            class Unit:

                def __init__(self):
                    self.kT = self.va = self.att = None
                    self.keys_in, self.values_in, self.result = [], [], []

            def attend_tile(d, b, w, w_in, rot_in, u, tt):
                wh, wl = w
                if tt == 0:
                    yield from need((keys, 1), (vals, 1))
                    u.kT, u.va = keys.take(), vals.take()
                while u.kT is None:
                    yield
                kT, va = u.kT, u.va
                yield from need((banks, 2, 0), (works, 3), (stats, 1))
                qk, vp = banks.take(), banks.take()
                st = stats.take()
                PE.wait(w_in, xs_mark[b], qk.free, vp.free)
                for c in range(C):
                    tok = slice(tt * P, (tt + 1) * P)
                    for x_, w_, n in ((xs_hi, wh, 0), (xs_hi, wl, 1), (xs_lo, wh, 2)):
                        first, last = c == 0 and n == 0, c == C - 1 and n == 2
                        ins = tensor.matmul(qk.ap, x_[:, c, b, tok], columns(w_, c, 0, 512), start=first, stop=last)
                        ins = tensor.matmul(vp.ap[:, 0:256], x_[:, c, b, tok], columns(w_, c, 512, 768), start=first, stop=last)
                t = pe_(ins)
                raw, t1, t2 = (works.take() for _ in range(3))
                A.wait(t, va.free, raw.free, t2.free)
                t_raw = a_(scalar.activation(raw.ap, qk.ap, ACT.Copy))
                t_sq = a_(scalar.activation(t2.ap, qk.ap, ACT.Square))
                banks.give(qk, t_sq)
                t_v = a_(scalar.activation(va.ap[:, tt, :], vp.ap[:, 0:256], ACT.Copy))
                banks.give(vp, t_v)
                yield
                yield
                v4 = lambda x, lo=0, hi=LHD: x.rearrange("p (s h d) -> p s h d", s=2, d=LHD)[:, :, :, lo:hi]
                v8 = lambda x: x.rearrange("p (h d) -> p h d", d=LHD)
                hd2 = LHD // 2
                G.wait(t_raw, t1.free, rot_in)
                t_t1 = g_(gpsimd.tensor_tensor(v4(t1.ap), v4(raw.ap), bc(rot.ap[:, 0, tt], 2, 4), ALU.mult))
                ss, y, tmp = st.ap[:, 0:8], st.ap[:, 8:16], st.ap[:, 16:24]
                V.wait(t_sq, st.free, rot_in)
                m = v_(vector.tensor_reduce(ss, v8(t2.ap), AX.X, ALU.add))
                V.wait(m)
                t_t2 = v_(vector.tensor_tensor(v4(t2.ap, 0, hd2), v4(raw.ap, hd2, LHD), bc(rot.ap[:, 1, tt, :, 0:hd2], 2, 4), ALU.mult))
                t_t2 = v_(vector.tensor_tensor(v4(t2.ap, hd2, LHD), v4(raw.ap, 0, hd2), bc(rot.ap[:, 1, tt, :, hd2:LHD], 2, 4), ALU.mult))
                works.give(raw, t_t1, t_t2)
                m = v_(vector.tensor_scalar(ss, ss, 1e-24, None, ALU.max))
                V.wait(m)
                t_y = rsqrt(ss, y, tmp)
                G.wait(t_t1, t_t2)
                m = g_(gpsimd.tensor_tensor(t1.ap, t1.ap, t2.ap, ALU.add))
                works.give(t2, m)
                G.wait(m, t_y)
                t_r = g_(gpsimd.tensor_tensor(v8(t1.ap), v8(t1.ap), bc(y, 2, LHD), ALU.mult))
                stats.give(st, t_r)
                yield
                yield
                while len(u.keys_in) < tt:
                    yield
                yield from need((banks, 1, 0), (queries, 1))
                ps, qz = banks.take(), queries.take()
                PE.wait(t_r, ps.free)
                for j in range(4):
                    ins = tensor.transpose(ps.ap[:, j * P:(j + 1) * P], t1.ap[:, j * P:(j + 1) * P], ident[:, :])
                t = pe_(ins)
                works.give(t1, t)
                A.wait(t, kT.free)
                t_k = a_(scalar.activation(kT.ap[:, :, PAD + tt * P:PAD + (tt + 1) * P], ps.ap[:, 2 * P:4 * P].rearrange("p (j n) -> p j n", j=2), ACT.Copy))
                V.wait(t_k, qz.free)
                for e in range(2):
                    r = slice(64 * e, 64 * e + 64)
                    A.wait(qz.free)
                    t_q = a_(scalar.activation(qz.ap[r, e:4:2, :], ps.ap[r, 0:2 * P].rearrange("p (j n) -> p j n", j=2), ACT.Copy))
                banks.give(ps, t_k, t_q)
                u.keys_in.append(t_k)
                u.values_in.append(t_v)
                yield
                yield from need((banks, 0, 1), (probs, 1), (stats, 1))
                ps, pr, st = banks.take(2), probs.take(), stats.take()
                f = 64 if tt else P
                PE.wait(t_k, t_q, ps.free)
                for h in range(4):
                    o = ps.ap[:, h // 2, (h % 2) * 256 + f:(h % 2) * 256 + 256]
                    tensor.matmul(o, qz.ap[:, h, :], kT.ap[:, h // 2, PAD + (tt - 1) * P + f:PAD + (tt + 1) * P], start=True, stop=False)
                    ins = tensor.matmul(o, ident_b[:, :], band[:, f:256], start=False, stop=True)
                t = pe_(ins)
                queries.give(qz, t)
                sc = ps.ap.rearrange("p b (h n) -> p (b h) n", h=2)
                V.wait(t, st.free)
                t = v_(vector.tensor_reduce(st.ap[:, 0:4], sc[:, :, f:256], AX.X, ALU.max, negate=True))
                yield
                A.wait(t, pr.free)
                for h in range(4):
                    t = a_(scalar.activation(pr.ap[:, h, f:256], sc[:, h, f:256], ACT.Exp, bias=st.ap[:, h:h + 1], accum_out=st.ap[:, 4 + h:5 + h]))
                banks.give(ps, t)
                V.wait(t)
                t = v_(vector.reciprocal(st.ap[:, 8:12], st.ap[:, 4:8]))
                yield
                A.wait(t)
                for h in range(4):
                    t_p = a_(scalar.activation(pr.ap[:, h, f:256], pr.ap[:, h, f:256], ACT.Copy, scale=st.ap[:, 8 + h:9 + h]))
                stats.give(st, t_p)
                yield
                js = (0, 1) if tt else (1,)
                PE.wait(t_p, u.values_in[tt])
                v2_ = lambda x: x.rearrange("p (h n) -> p h n", h=2)[:, :, js[0] * P:2 * P]
                copies = []
                yield from need((banks, 2, 0), (turned, 2))
                for pair in range(2):
                    ps, pt = banks.take(), turned.take()
                    PE.wait(ps.free)
                    for hh in range(2):
                        for j in js:
                            n0 = (2 * hh + j) * P
                            ins = tensor.transpose(ps.ap[:, n0:n0 + P], pr.ap[:, 2 * pair + hh, j * P:(j + 1) * P], ident[:, :])
                    t_pt = pe_(ins)
                    V.wait(t_pt, pt.free)
                    t = v_(vector.tensor_copy(v2_(pt.ap), v2_(ps.ap)))
                    banks.give(ps, t)
                    copies.append((pt, t))
                probs.give(pr, t_pt)
                yield
                if u.att is None:
                    yield from need((pairs, 1))
                    u.att = pairs.take()
                yield from need((banks, 1, 0))
                acc = banks.take()
                PE.wait(acc.free)
                for pair, (pt, t) in enumerate(copies):
                    PE.wait(t)
                    for j in js:
                        for hh in range(2):
                            hd = (2 * pair + hh) * LHD
                            n0 = (2 * hh + j) * P
                            ins = tensor.matmul(acc.ap[64 * hh:64 * hh + 64, pair * P:(pair + 1) * P], va.ap[:, tt - 1 + j, hd:hd + LHD],
                                                pt.ap[:, n0:n0 + P], start=j == js[0], stop=j == 1)
                    t = pe_(ins)
                    turned.give(pt, t)
                hi, lo = u.att.ap
                o2 = acc.ap[:, 0:2 * P].rearrange("p (j n) -> p j n", j=2)
                tok = slice(tt * P, (tt + 1) * P)
                A.wait(t, u.att.free)
                t = a_(scalar.activation(hi[:, :, tok], o2, ACT.Copy))
                V.wait(t, u.att.free)
                t_o = v_(vector.tensor_tensor(lo[:, :, tok], o2, hi[:, :, tok].bitcast(F32), ALU.subtract))
                banks.give(acc, t_o)
                u.result.append((tt, t_o))
                yield

            def add_attended(b, w, u, done):
                wh, wl = w
                while len(u.result) < QT:
                    yield
                yield
                hi, lo = u.att.ap
                keys.give(u.kT, (PE.sem, PE.n))
                vals.give(u.va, (PE.sem, PE.n))
                xs_read[b].append((PE.sem, PE.n))
                for m in range(C):
                    yield from need((banks, 1, 0))
                    ps = banks.take()
                    PE.wait(ps.free, [t for _, t in u.result])
                    for k in range(2):
                        at_ = C * COLS + k * D + m * P
                        ins = split3(ps.ap, wh[:, at_:at_ + P], wl[:, at_:at_ + P], hi[:, k, :], lo[:, k, :], k == 0, k == 1)
                    t = pe_(ins)
                    V.wait(t, x_ready[b], xs_mark[b])
                    t = v_(vector.tensor_tensor(tokens(b, m), ps.ap, tokens(b, m), ALU.add))
                    banks.give(ps, t)
                x_ready[b] = [t]
                pairs.give(u.att, (PE.sem, PE.n))
                done.append((PE.sem, PE.n))

            def feed_forward3(d, b, w_in, done):
                wh, wl = w12.ap
                yield from need((keys, 1), (pairs, 1))
                xc, xn = keys.take(), pairs.take()
                rstd, t_rs = yield from centred_rstd(b, 1, xc, works)
                hi, lo = xn.ap
                V.wait(t_rs)
                for c in range(C):
                    t = v_(vector.scalar_tensor_tensor(out=xc.ap[:, c, PAD:ROW], in0=xc.ap[:, c, PAD:ROW], scalar=sm(f"ln_gr{d}", c),
                                                       in1=rstd.ap, op0=ALU.mult, op1=ALU.mult))
                works.give(rstd, t)
                A.wait(t, xn.free)
                V.wait(t, xn.free)
                for c in range(C):
                    t = a_(scalar.activation(hi[:, c, :], xc.ap[:, c, PAD:ROW], ACT.Identity, bias=vec(f"ln_b{d}", c)))
                    V.wait(t)
                    t_xn = v_(vector.scalar_tensor_tensor(out=lo[:, c, :], in0=xc.ap[:, c, PAD:ROW], scalar=vec(f"ln_b{d}", c),
                                                          in1=hi[:, c, :].bitcast(F32), op0=ALU.add, op1=ALU.subtract))
                keys.give(xc, t_xn)
                yield
                yield from need((banks, 2, 0))
                acc = [banks.take() for _ in range(C)]
                PE.wait(w_in, t_xn, acc[0].free, acc[1].free)
                before = None
                for i in range(HT + 1):
                    if i < HT:
                        yield from need((banks, 2, 0), (works, 2))
                        pa, pg, g, h = banks.take(), banks.take(), works.take(), works.take()
                        PE.wait(pa.free, pg.free)
                        for ps, k in ((pg, 2 * i + 1), (pa, 2 * i)):
                            for c in range(C):
                                at_ = c * 2 * HT * P + k * P
                                ins = split3(ps.ap, wh[:, at_:at_ + P], wl[:, at_:at_ + P], hi[:, c, :], lo[:, c, :], c == 0, c == C - 1)
                            t = pe_(ins)
                            if ps is pg:
                                A.wait(t, g.free)
                                t_g = a_(scalar.activation(g.ap, pg.ap, ACT.Gelu, bias=vec(f"b1g{d}", i)))
                                banks.give(pg, t_g)
                        V.wait(t, t_g, h.free)
                        t = v_(vector.scalar_tensor_tensor(out=h.ap, in0=pa.ap, scalar=vec(f"b1a{d}", i), in1=g.ap, op0=ALU.add, op1=ALU.mult))
                        banks.give(pa, t)
                        works.give(g, t)
                        t_gated = t
                    if before is not None:
                        k, hb, t_hb = before
                        PE.wait(t_hb)
                        for m in range(C):
                            at_ = C * 2 * HT * P + k * D + m * P
                            ins = split3(acc[m].ap, wh[:, at_:at_ + P], wl[:, at_:at_ + P], hb.ap[0][:, :], hb.ap[1][:, :], k == 0, k == HT - 1)
                        t = pe_(ins)
                        hids.give(hb, t)
                    if i < HT:
                        yield from need((hids, 1))
                        hid = hids.take()
                        V.wait(t_gated, hid.free)
                        t_hi = v_(vector.tensor_copy(hid.ap[0][:, :], h.ap))
                        G.wait(t_hi)
                        t_h = g_(gpsimd.tensor_tensor(hid.ap[1][:, :], h.ap, hid.ap[0][:, :].bitcast(F32), ALU.subtract))
                        works.give(h, t_h)
                        before = (i, hid, t_h)
                    yield
                pairs.give(xn, (PE.sem, PE.n))
                V.wait(t)
                for m in range(C):
                    t_x = v_(vector.scalar_tensor_tensor(out=tokens(b, m), in0=acc[m].ap, scalar=vec(f"b2{d}", m), in1=tokens(b, m),
                                                         op0=ALU.add, op1=ALU.add))
                    banks.give(acc[m], t_x)
                x_ready[b] = [t_x]
                xs_read[b] = xs_read[b][-4:]
                if d < depths - 1:
                    split_tokens(b)
                    xs_read[b] = []
                done.append((PE.sem, PE.n))
                yield

            for b in range(B):
                split_tokens(b)

            jobs, turn = [], [0] * B

            def filled(box):
                while not box:
                    yield

            quad_in, rot_box, ff_in, used_ff, used_quads = {}, {}, {}, {-1: []}, {}

            def load_quad(d, g):
                yield from need((quads, 1))
                q_ = quads.take()
                box = []
                yield from load_split(q_.ap, a["quads"][d, g], QW, q_.free, box)
                quad_in[d, g] = (q_, box[0])

            def load_ff(d):
                while d and len(used_ff[d - 1]) < B:
                    yield
                box = []
                yield from load_split(w12.ap, a["w12"][d], FW, used_ff[d - 1], box)
                ff_in[d] = box[0]

            def make_tables(d):
                while d and sum(attended[d - 1, b] for b in range(B)) < 4 * B:
                    yield
                box = []
                yield from rotary_tables(d, [(G.sem, G.n)], box)
                rot_box[d] = box[0]

            def tile(d, g, b, u, tt):
                while (d, g) not in quad_in or d not in rot_box or turn[b] < 2 * d:
                    yield
                q_, w_in = quad_in[d, g]
                yield from attend_tile(d, b, q_.ap, w_in, rot_box[d], u, tt)

            def finish_unit(d, g, b, u):
                while (d, g) not in quad_in:
                    yield
                q_, _ = quad_in[d, g]
                yield from add_attended(b, q_.ap, u, used_quads[d, g])
                if len(used_quads[d, g]) == B:
                    quads.give(q_, *used_quads[d, g])
                attended[d, b] += 1
                if attended[d, b] == 4:
                    turn[b] = 2 * d + 1

            def ff(d, b):
                while d not in ff_in or turn[b] < 2 * d + 1:
                    yield
                yield from feed_forward3(d, b, ff_in[d], used_ff[d])
                turn[b] = 2 * d + 2

            attended = {(d, b): 0 for d in range(depths) for b in range(B)}
            for d in range(depths):
                used_ff[d] = []
                for g in range(4):
                    used_quads[d, g] = []
                if d == 0:
                    jobs += [load_quad(0, 0), make_tables(0)]
                for g in range(4):
                    for b in range(B):
                        if b == 2:
                            jobs.append(load_quad(d, g + 1) if g < 3 else load_ff(d))
                        u = Unit()
                        jobs += [tile(d, g, b, u, tt) for tt in range(QT)] + [finish_unit(d, g, b, u)]
                for b in range(B):
                    if b == 1 and d < depths - 1:
                        jobs += [make_tables(d + 1), load_quad(d + 1, 0)]
                    jobs.append(ff(d, b))
            run_jobs(jobs, W2_JOBS)

        if stages >= 8:
            with ExitStack() as p2:
                last_part(p2)

        s_out = sem("out_written")
        with ExitStack() as p3:
            if stages >= 8:
                V.wait((PE.sem, PE.n), (A.sem, A.n), (G.sem, G.n), (V.sem, V.n))
                SP.wait((PE.sem, PE.n), (A.sem, A.n), (G.sem, G.n), (V.sem, V.n), *kept)
                back = sb("x_back", [P, C, B, S], F32, p3)
            for b in range(B):
                t = x_ready[b]
                if stages >= 8:
                    s_back = sem(f"back{b}")
                    for c in range(C):
                        sync.dma_start(back[:, c, b, :], x_kept[c * P:(c + 1) * P, b, :]).then_inc(s_back, 16)
                    V.wait(x_ready[b], (s_back, 16 * C))
                    for c in range(C):
                        t = v_(vector.scalar_tensor_tensor(out=back[:, c, b, :], in0=tokens(b, c), scalar=gates[:, 7:8],
                                                           in1=back[:, c, b, :], op0=ALU.mult, op1=ALU.add))
                SP.wait(t)
                for c in range(C):
                    src = back[:, c, b, :] if stages >= 8 else tokens(b, c)
                    sync.dma_start(out[c * P:(c + 1) * P, b, :], src).then_inc(s_out, 16)
        sync.wait_ge(s_out, 16 * C * B)


def _layout(x):
    n = x.shape[0] // P
    return np.ascontiguousarray(x.reshape(n, P, -1).transpose(1, 0, 2).reshape(P, -1))


def lay_out(i):
    i = {k: np.asarray(v) for k, v in i.items()}
    col = lambda v: np.ascontiguousarray(v.reshape(-1, P).T)
    rep = lambda v: np.broadcast_to(v.reshape(1, -1), (P, v.size))
    a = {}
    a["xT"] = np.ascontiguousarray(i["x"].transpose(2, 0, 1))
    a["ctxT"] = np.ascontiguousarray(i["ctx_1024"].transpose(2, 0, 1))
    a["ctx"] = np.ascontiguousarray(i["ctx_1024"])
    m = i["mask_BxSxS2_bf1"]
    a["mask"] = np.ascontiguousarray(m).view(np.uint8)
    a["maskT"] = np.ascontiguousarray(m.transpose(0, 2, 1)).view(np.uint8)

    def att(L, wq, wk, wv, wo):
        wop = np.zeros((H, 32, D), np.float32)
        wop[:, :HD] = wo.reshape(H, HD, D)
        a[L] = np.ascontiguousarray(np.concatenate([_layout(wq), _layout(wk), _layout(wv), _layout(wop.reshape(H * 32, D))], 1))

    flat = lambda w: w.transpose(1, 0, 2).reshape(D, D)
    att("L0_att", *(i[f"L0_xattn_w{n}"].T for n in "qkvo"))
    att("L1_att", *(flat(i[f"L1_xattn_W{n}"]) for n in "qkv"), i["L1_xattn_Wo"])
    att("L3_att", *(i[f"L3_xattn_W{n}"].T for n in "qkvo"))
    a["L0_ff"] = np.ascontiguousarray(np.concatenate([_layout(i["L0_ffn_w1"].T), _layout(i["L0_ffn_w2"].T)], 1))
    a["L1f_w"] = _layout(i["L1_ffn_kernel"]).reshape(P, C, D)
    a["L1f_bias"] = col(i["L1_ffn_bias"])
    a["L2_att"] = _layout(i["L2_xattn_W"].T)
    a["L2_ff"] = np.ascontiguousarray(np.concatenate([_layout(i[f"L2_ffn_W_{n}"].T) for n in "rkv"], 1))
    a["bv"] = np.ascontiguousarray(np.stack([rep(i[f"{L}_xattn_bv"]) for L in ("L0", "L1", "L3")], 1))
    cols = {
        "L0_b1": col(i["L0_ffn_b1"]), "L0_b2": col(i["L0_ffn_b2"]), "L2_b": col(i["L2_xattn_b"]),
        "mu_r": col(i["L2_ffn_mu_r"]), "mu_k": col(i["L2_ffn_mu_k"]),
        "g_x": rep(i["g_xattn"]), "g_f": rep(i["g_ffn"]),
        "s_in": rep(i["L1_ffn_input_scale"]), "s_k": rep(i["L1_ffn_kernel_scale"]),
    }
    for L in ("L0", "L1", "L3"):
        for n in "qko":
            cols[f"{L}_b{n}"] = col(i[f"{L}_xattn_b{n}"])
    pad = lambda v: np.concatenate([v, np.zeros(HT * P - HID, np.float32)])
    for d in range(DEPTH):
        cols[f"ln_g{d}"], cols[f"ln_b{d}"] = col(i["L3_ffn_ln_g"][d]), col(i["L3_ffn_ln_b"][d])
        cols[f"b1a{d}"], cols[f"b1g{d}"] = col(pad(i["L3_ffn_b1"][d][:HID])), col(pad(i["L3_ffn_b1"][d][HID:]))
        cols[f"b2{d}"] = col(i["L3_ffn_b2"][d])
    a["vecs"] = np.zeros((P, N_VECS), np.float32)
    for name, at in VECS.items():
        a["vecs"][:, at:at + cols[name].shape[1]] = cols[name]
    a["ident"] = np.eye(P, dtype=np.float32)
    bf16 = i["L1_ffn_kernel"].dtype
    a["ones"] = np.ones((2, 4 * S2), bf16)
    n, h = S, LHD // 2
    half = np.arange(0, LHD, 2, dtype=np.float32)
    t = np.arange(n, dtype=np.float32)
    freqs = t[:, None] * (1.0 / 10000.0 ** (half / LHD)).astype(np.float32)[None]
    power = (t - n // 2) / (WIN // 2)
    scale = ((half + 0.4 * LHD) / (1.4 * LHD)).astype(np.float32)[None] ** power[:, None]
    cos, sin = np.cos(freqs), np.sin(freqs)
    tab = np.zeros((2, n, 2, LHD), np.float32)
    for j, f in enumerate((-8.0 * RSQRT * scale, -RSQRT / scale)):
        tab[0, :, j] = np.concatenate([cos * f, cos * f], 1)
        tab[1, :, j] = np.concatenate([-sin * f, sin * f], 1)
    a["rotary"] = np.ascontiguousarray(tab.reshape(2, QT, P, 2, LHD).transpose(2, 0, 1, 3, 4))
    back = np.arange(P)[:, None] - (np.arange(2 * P)[None] - P)
    a["band"] = np.where((back >= 0) & (back <= WIN), 0.0, MASKED).astype(bf16)
    qs = np.stack([i["L3_ffn_q_scale"], i["L3_ffn_k_scale"]], 1)
    a["qk_scale"] = np.ascontiguousarray(np.broadcast_to(qs[:, None], (DEPTH, P, 2, LHD)))
    wqkv = i["L3_ffn_Wqkv"].reshape(DEPTH, D, 3, 4, 4 * LHD).transpose(0, 3, 1, 2, 4).reshape(DEPTH, 4, D, 12 * LHD)
    wo = i["L3_ffn_Wo"].reshape(DEPTH, 4, 4 * LHD, D)
    a["quads"] = np.stack([np.stack([np.concatenate([_layout(wqkv[d, g]), _layout(wo[d, g])], 1) for g in range(4)]) for d in range(DEPTH)])
    w1 = np.zeros((DEPTH, D, HT, 2, P), np.float32)
    w2 = np.zeros((DEPTH, HT * P, D), np.float32)
    for k in range(2):
        w = np.zeros((DEPTH, D, HT * P), np.float32)
        w[:, :, :HID] = i["L3_ffn_W1"][:, :, k * HID:(k + 1) * HID]
        w1[:, :, :, k] = w.reshape(DEPTH, D, HT, P)
    w2[:, :HID] = i["L3_ffn_W2"]
    a["w12"] = np.stack([np.concatenate([_layout(w1[d].reshape(D, -1)), _layout(w2[d])], 1) for d in range(DEPTH)])
    return a


def kernel(**inputs):
    import concourse.bacc as _bacc
    from concourse.bass_utils import run_bass_kernel_spmd as _run

    nc = _bacc.Bacc("TRN2", target_bir_lowering=False, num_devices=1)
    arrays = {f"in_{k}": v for k, v in lay_out(inputs).items()}
    aps = {k[3:]: nc.dram_tensor(k, v.shape, mybir.dt.from_np(v.dtype), kind="ExternalInput").ap() for k, v in arrays.items()}
    out = nc.dram_tensor("out_xT", (D, B, S), F32, kind="ExternalOutput").ap()
    build(nc, aps, out)
    r = _run(nc, [arrays], core_ids=[0])
    return np.ascontiguousarray(r.results[0]["out_xT"].transpose(1, 2, 0))
```
